# Optimizing a Trainium2 kernel written in Bass

```python
import numpy as np
import jax
import jax.numpy as jnp

def _softmax(x, axis=-1):
    return jax.nn.softmax(x, axis=axis)

def _gelu(x):
    return jax.nn.gelu(x, approximate=True)

def _silu(x):
    return jax.nn.silu(x)

def _sigmoid(x):
    return jax.nn.sigmoid(x)

def _layernorm(x, axis=-1, eps=1e-05):
    m = jnp.mean(x, axis=axis, keepdims=True)
    v = jnp.var(x, axis=axis, keepdims=True)
    return (x - m) / jnp.sqrt(v + eps)

def _scatter_add(tgt, idx, src, axis=0):
    return tgt.at[idx].add(src)

def _segment_sum(src, seg, n):
    return jax.ops.segment_sum(src, seg, n)
kernel_name = 'mk_adj_preln_d2_adj_r2_e89660'

def setup_inputs(seed: int=0):
    np.random.seed(seed)
    _w = jnp.asarray

    def _rec_inputs():
        import jax
        import jax.numpy as jnp
        _gk = jax.random.key(seed)
        x = 7.22e-05 + 1 * jax.random.normal(jax.random.fold_in(_gk, 1), (32, 256, 512), jnp.float32)
        _w = (1.0 + jnp.arange(256, dtype=jnp.float32)) ** (-0.5)
        _w = _w / _w.mean()
        _pij = jnp.clip(0.015625 * _w[:, None] * _w[None, :], 0.0, 1.0)
        _a = jax.random.uniform(jax.random.fold_in(_gk, 2), (32, 256, 256)) < _pij
        _a = jnp.logical_or(_a, jnp.eye(256, dtype=bool))
        adj = _a.astype(jnp.int32)
        return (x, adj)
    x, adj = _rec_inputs()

    def _L0_gnn_setup():
        import jax, jax.numpy as jnp
        import numpy as np
        import math
        D_MODEL = 512
        N_HEADS = 16
        D_HEAD = D_MODEL // N_HEADS
        B, S = (4, 1024)
        key = jax.random.key(seed)
        ks = jax.random.split(key, 10)
        x = jax.random.normal(ks[0], (B, S, D_MODEL), dtype=jnp.float32)
        mask = jax.random.randint(ks[1], (B, S, S), 0, 2, dtype=jnp.int32)
        eye = jnp.eye(S, dtype=jnp.int32)[None]
        mask = jnp.maximum(mask, eye)
        std = 1.0 / math.sqrt(D_MODEL)
        Wq = jax.random.normal(ks[2], (D_MODEL, D_MODEL), dtype=jnp.float32) * std
        Wk = jax.random.normal(ks[3], (D_MODEL, D_MODEL), dtype=jnp.float32) * std
        Wv = jax.random.normal(ks[4], (D_MODEL, D_MODEL), dtype=jnp.float32) * std
        Wo = jax.random.normal(ks[5], (D_MODEL, D_MODEL), dtype=jnp.float32) * std
        bq = jnp.zeros((D_MODEL,), dtype=jnp.float32)
        bk = jnp.zeros((D_MODEL,), dtype=jnp.float32)
        bv = jnp.zeros((D_MODEL,), dtype=jnp.float32)
        bo = jnp.zeros((D_MODEL,), dtype=jnp.float32)
        return {'x': x, 'mask': mask, 'Wq': Wq, 'bq': bq, 'Wk': Wk, 'bk': bk, 'Wv': Wv, 'bv': bv, 'Wo': Wo, 'bo': bo}
    _L0_gnn_all = _L0_gnn_setup()
    _L0_gnn_in = {k: v for k, v in _L0_gnn_all.items() if k in ('Wq', 'bq', 'Wk', 'bk', 'Wv', 'bv', 'Wo', 'bo')}
    del _L0_gnn_all

    def _L1_gnn_setup():
        import jax, jax.numpy as jnp
        import numpy as np
        IN_DIM = 512
        OUT_DIM = 512
        BATCH = 128
        NUM_OBJS = 100
        key = jax.random.key(seed)
        k1, k2, k3, k4, k5 = jax.random.split(key, 5)
        stdv = 1.0 / np.sqrt(OUT_DIM)
        feature = jax.random.normal(k1, (BATCH, NUM_OBJS, IN_DIM), dtype=jnp.float32)
        graph = jax.random.randint(k2, (BATCH, NUM_OBJS, NUM_OBJS), 0, 2, dtype=jnp.int32)
        weight = jax.random.uniform(k3, (IN_DIM, OUT_DIM), dtype=jnp.float32, minval=-stdv, maxval=stdv)
        wq = jax.random.uniform(k4, (IN_DIM, OUT_DIM), dtype=jnp.float32, minval=-stdv, maxval=stdv)
        wk = jax.random.uniform(k5, (IN_DIM, OUT_DIM), dtype=jnp.float32, minval=-stdv, maxval=stdv)
        return {'feature': feature, 'graph': graph, 'weight': weight, 'wq': wq, 'wk': wk}
    _L1_gnn_all = _L1_gnn_setup()
    _L1_gnn_in = {k: v for k, v in _L1_gnn_all.items() if k in ('weight', 'wq', 'wk')}
    del _L1_gnn_all
    return {'x': x, 'adj': adj, 'L0_gnn_Wq': _L0_gnn_in['Wq'], 'L0_gnn_bq': _L0_gnn_in['bq'], 'L0_gnn_Wk': _L0_gnn_in['Wk'], 'L0_gnn_bk': _L0_gnn_in['bk'], 'L0_gnn_Wv': _L0_gnn_in['Wv'], 'L0_gnn_bv': _L0_gnn_in['bv'], 'L0_gnn_Wo': _L0_gnn_in['Wo'], 'L0_gnn_bo': _L0_gnn_in['bo'], 'L1_gnn_weight': _L1_gnn_in['weight'], 'L1_gnn_wq': _L1_gnn_in['wq'], 'L1_gnn_wk': _L1_gnn_in['wk']}

def reference(x, adj, L0_gnn_Wq, L0_gnn_bq, L0_gnn_Wk, L0_gnn_bk, L0_gnn_Wv, L0_gnn_bv, L0_gnn_Wo, L0_gnn_bo, L1_gnn_weight, L1_gnn_wq, L1_gnn_wk):
    import jax
    import jax.numpy as jnp

    def _L0_gnn_ref(x, mask, Wq, bq, Wk, bk, Wv, bv, Wo, bo):
        import jax, jax.numpy as jnp
        import numpy as np
        import math
        D_MODEL = 512
        N_HEADS = 16
        D_HEAD = D_MODEL // N_HEADS
        B, S = (4, 1024)
        b, s, _ = x.shape
        scale = 1.0 / math.sqrt(D_HEAD)

        def heads(t):
            return t.reshape(b, s, N_HEADS, D_HEAD).transpose(0, 2, 1, 3)
        q = heads(x @ Wq + bq)
        k = heads(x @ Wk + bk)
        v = heads(x @ Wv + bv)
        scores = jnp.einsum('bhqd,bhkd->bhqk', q, k) * scale
        scores = jnp.where(mask[:, None] == 0, -jnp.inf, scores)
        attn = jax.nn.softmax(scores, axis=-1)
        out = jnp.einsum('bhqk,bhkd->bhqd', attn, v)
        out = out.transpose(0, 2, 1, 3).reshape(b, s, D_MODEL)
        return out @ Wo + bo

    def _L1_gnn_ref(feature, graph, weight, wq, wk):
        import jax, jax.numpy as jnp
        import numpy as np
        IN_DIM = 512
        OUT_DIM = 512
        BATCH = 128
        NUM_OBJS = 100
        output = jnp.einsum('bni,io->bno', feature, weight)
        q = jnp.einsum('bni,io->bno', feature, wq)
        k = jnp.einsum('bni,io->bno', feature, wk)
        alpha = jnp.einsum('bno,bmo->bnm', q, k)
        alpha = jnp.maximum(alpha, 0.0) * (graph != 0).astype(alpha.dtype)
        alpha = jax.nn.softmax(alpha, axis=1)
        return jnp.einsum('bnm,bmo->bno', alpha, output)
    h = jnp.maximum(_layernorm(x, axis=-1), 0.0)
    x = x + _L0_gnn_ref(h, adj, L0_gnn_Wq, L0_gnn_bq, L0_gnn_Wk, L0_gnn_bk, L0_gnn_Wv, L0_gnn_bv, L0_gnn_Wo, L0_gnn_bo)
    h = jnp.maximum(_layernorm(x, axis=-1), 0.0)
    x = x + _L1_gnn_ref(h, adj, L1_gnn_weight, L1_gnn_wq, L1_gnn_wk)
    return x

_drawn_inputs = setup_inputs


def setup_inputs(seed=0):
    import zlib

    import numpy as np

    out = dict(_drawn_inputs(seed))
    spreads = {'L0_gnn_bq': (0.0, 0.641),
     'L0_gnn_bk': (0.0, 0.8),
     'L0_gnn_bv': (0.0, 0.1),
     'L0_gnn_bo': (0.0, 0.1)}
    factors = {}
    for name, (base, spread) in spreads.items():
        noise = np.random.default_rng([zlib.crc32(name.encode()), seed]).standard_normal(out[name].shape)
        drawn = base * np.exp(spread * noise) if base else spread * noise
        out[name] = jnp.asarray(drawn.astype(out[name].dtype))
    for name, factor in factors.items():
        out[name] = (out[name] * factor).astype(out[name].dtype)
    return out
```

```python
import concourse.bass as bass
from concourse import mybir
from contextlib import ExitStack

BATCH, NODES, DIM, HEADS = 32, 256, 512, 16
HEAD = DIM // HEADS
P = 128
KT = DIM // P
QT = NODES // P
GROUP = P // HEAD
VCOLS = 3 * HEAD + 1
VPITCH = VCOLS + 1
SCALE = HEAD ** -0.5
EPS = 1e-5
FAR = 3.0e38
RSQRT_SEED = 0x5F3759DF
NEWTON_ROUNDS = 3
NSTEPS = 3 + 4 * NEWTON_ROUNDS

DENSE = [
    ["v1"],
    ["ot1", "qk2"],
    ["wo0"],
    ["wo1"],
    [],
    ["qk3"],
    ["h2_0", "h2_1", "hw0"],
    ["g0"],
    ["g1"],
    ["h1_0", "h1_1", "hw1"],
    ["qk0"],
    ["al"],
    [],
    ["av0"],
    ["av1", "qk1"],
    ["ot0", "v0"],
]
RING = 3
ORDER = [name for step in DENSE for name in step]
assert len(ORDER) % RING == 0 and len(DENSE) == HEADS
ROLE = {"v1": 0, "ot1": -1, "qk2": 0, "wo0": -1, "wo1": -1, "qk3": 0, "h2_0": -1, "h2_1": -1,
        "hw0": -1, "g0": -1, "g1": -1, "h1_0": 1, "h1_1": 1, "hw1": -1, "qk0": 1, "al": -1,
        "av0": -1, "av1": -1, "qk1": 1, "ot0": 0, "v0": 1}
BANK = {name: i % RING for i, name in enumerate(ORDER)}


def count(graph, per_graph, k):
    return graph * per_graph + (k + 1)


def started(graph):
    return not (isinstance(graph, int) and graph < 0)


def bank_before(name, t):
    at, shift = ORDER.index(name), 0
    while True:
        at -= RING
        if at < 0:
            at, shift = at + len(ORDER), shift - 1
        other = ORDER[at]
        graph = t + shift + ROLE[other]
        if t + shift < -1:
            return None, 0
        if 0 <= graph < BATCH:
            return other, graph - t


def two_layers(nc, x, adj, adj_t, wq, wk, wv, wo, bq, bk, bv, bo, w1, wq1_t, wk1_t, out):
    f32, f32r = mybir.dt.float32, mybir.dt.float32r
    bf16, f16, i32 = mybir.dt.bfloat16, mybir.dt.float16, mybir.dt.int32
    ALU, ACT, AX = mybir.AluOpType, mybir.ActivationFunctionType, mybir.AxisListType

    x_v = x.rearrange("b (q p) d -> b p q d", p=P)
    out_v = out.rearrange("b (q p) d -> b p q d", p=P)
    adj_v = adj.rearrange("b (q p) k -> b p q k", p=P)
    adjt_v = adj_t.rearrange("b (q p) k -> b p q k", p=P)

    ctx = ExitStack()
    with ctx:
        def sb(name, shape, dt):
            return ctx.enter_context(nc.sbuf_tensor(name, shape, dt))

        def bank(name):
            return ctx.enter_context(nc.psum_tensor(name, [P, 512], f32))

        def sem(name):
            return ctx.enter_context(nc.semaphore(name))

        WH = {n: sb(f"{n}_hi", [P, KT, DIM], f32r) for n in ("wq", "wk", "wv", "wo", "wm", "w1")}
        WL = {n: sb(f"{n}_lo", [P, KT, DIM], f32r) for n in ("wq", "wk", "wv", "wo", "wm", "w1")}
        ident = sb("ident", [P, P], f32)
        bias_q = sb("bias_q", [P, KT], f32)
        bias_k = sb("bias_k", [P, KT], f32)
        bias_v = sb("bias_v", [P, KT], f32)
        out_bias = sb("out_bias", [P, DIM], f32)

        xa = sb("xa", [P, QT, DIM], f32)
        x1 = sb("x1", [P, QT, DIM], f32)
        adj_in = sb("adj_in", [P, QT, NODES], i32)
        adjt_in = sb("adjt_in", [P, QT, NODES], i32)
        far_next = sb("far_next", [P, QT, NODES], bf16)
        far = sb("far", [P, QT, NODES], bf16)
        keep = sb("keep", [P, QT, NODES], bf16)
        h1H = sb("h1_hi", [P, KT, NODES], f32r)
        h1L = sb("h1_lo", [P, KT, NODES], f32r)
        stage = sb("stage", [P, 2, 4, NODES], f32r)
        stack = sb("stack", [P, 2, GROUP, 2, NODES], f32r)
        val = sb("val", [P, QT, HEADS, VPITCH], bf16)
        v_rest = sb("v_rest", [P, QT, NODES], f32)
        probs = sb("probs", [P, 2, QT, NODES], f32)
        least = sb("least", [P, 2, QT], f32)
        pH = sb("probs_t_hi", [P, 2, QT, NODES], f16)
        pL = sb("probs_t_lo", [P, 2, QT, NODES], f16)
        o_sum = sb("o_sum", [P, 2, 4, HEAD], f32)
        o_rcp = sb("o_rcp", [P, 2, 4], f32)
        heads_out = sb("heads_out", [P, QT, DIM], f32)
        oH = sb("heads_t_hi", [P, KT, NODES], f32r)
        oL = sb("heads_t_lo", [P, KT, NODES], f32r)
        work = sb("work", [P, QT, DIM], f32)
        h2H = sb("h2_hi", [P, KT, NODES], f32r)
        h2L = sb("h2_lo", [P, KT, NODES], f32r)
        gH = sb("g_hi", [P, KT, NODES], f32r)
        gL = sb("g_lo", [P, KT, NODES], f32r)
        hwH = sb("hw_hi", [P, QT, DIM], f32r)
        hwL = sb("hw_lo", [P, QT, DIM], f32r)
        eH = sb("e_hi", [P, QT, NODES], f32r)
        eL = sb("e_lo", [P, QT, NODES], f32r)
        l1_max = sb("l1_max", [P, QT], f32)
        l1_sum = sb("l1_sum", [P, QT], f32)
        l1_rcp = sb("l1_rcp", [P, QT], f32)
        stats = [sb(f"stats{n}", [P, QT, 6], f32) for n in (1, 2)]
        meanvar = [sb(f"meanvar{n}", [P, QT, 2], f32) for n in (1, 2)]
        rstd = [sb(f"rstd{n}", [P, QT], f32) for n in (1, 2)]
        newton = [sb(f"newton{n}", [P, 3, QT], f32) for n in (1, 2)]

        score = [bank("score0"), bank("score1")]
        turned = [bank("turned0"), bank("turned1")]
        pv = bank("pv")
        ring = [bank(f"ring{i}") for i in range(RING)]
        pv4 = pv[:, 0:4 * VPITCH].rearrange("p (g c) -> p g c", c=VPITCH)

        xa_in, x1_in = sem("xa_in"), sem("x1_in")
        adj_got, adjt_got = sem("adj_got"), sem("adjt_got")
        stacked = [sem("stacked_even"), sem("stacked_odd")]
        stored = sem("stored")
        small_in = sem("small_in")
        chunk_in = [sem(f"chunk_in{i}") for i in range(3)]
        ident_ok, ones_ok = sem("ident_ok"), sem("ones_ok")
        w_high, w_low = sem("w_high"), sem("w_low")
        bv_high, bv_low = sem("bv_high"), sem("bv_low")
        bias_row, merged = sem("bias_row"), sem("merged")
        merged_hi, merged_lo = sem("merged_hi"), sem("merged_lo")
        bias_q_ok, bias_ok = sem("bias_q_ok"), sem("bias_ok")
        mm = {n: sem(f"mm_{n}") for n in
              ("h1", "qk", "v", "score", "turn", "pv", "ot", "wo", "h2", "g", "al", "hw", "av")}
        hi = {n: sem(f"hi_{n}") for n in ("h1", "qk", "v", "p", "ot", "h2", "g", "e", "hw")}
        v_mid, exped, l1_exped = sem("v_mid"), sem("exped"), sem("l1_exped")
        lo = {n: sem(f"lo_{n}") for n in ("h1", "qk", "v", "p", "ot", "h2", "g", "e", "hw")}
        masked, summed = sem("masked"), sem("summed")
        added, l1_masked, l1_maxed, l1_rcped, final = (
            sem("added"), sem("l1_masked"), sem("l1_maxed"), sem("l1_rcped"), sem("final"))
        stat = [sem("stat1"), sem("stat2")]
        var_ok = [sem("var_ok1"), sem("var_ok2")]
        normed = [sem("normed1"), sem("normed2")]
        far_ok = sem("far_ok")
        v_low, head_ok = sem("v_low"), sem("head_ok")
        nstep = [sem("nstep1"), sem("nstep2")]
        dve_settled, pool_settled = sem("dve_settled"), sem("pool_settled")
        x1_ok, keep_ok, far_next_ok = sem("x1_ok"), sem("keep_ok"), sem("far_next_ok")

        RELEASE = {"v1": (lo["v"], 2, 1), "v0": (lo["v"], 2, 0),
                   "ot0": (lo["ot"], 2, 0), "ot1": (lo["ot"], 2, 1),
                   "wo0": (added, 2, 0), "wo1": (added, 2, 1),
                   "h1_0": (lo["h1"], 2, 0), "h1_1": (lo["h1"], 2, 1),
                   "h2_0": (lo["h2"], 2, 0), "h2_1": (lo["h2"], 2, 1),
                   "g0": (lo["g"], 2, 0), "g1": (lo["g"], 2, 1), "al": (l1_masked, 1, 0),
                   "hw0": (lo["hw"], 2, 0), "hw1": (lo["hw"], 2, 1),
                   "av0": (final, 2, 0), "av1": (final, 2, 1),
                   "qk0": (lo["qk"], 4, 0), "qk1": (lo["qk"], 4, 1),
                   "qk2": (lo["qk"], 4, 2), "qk3": (lo["qk"], 4, 3)}

        CHUNKS = [(src, slot, factor, half)
                  for src, slot, factor in ((wk1_t, "wo", None), (wq1_t, "w1", None),
                                            (wq, "wq", -SCALE), (wk, "wk", None), (wv, "wv", None),
                                            (wo, "wo", None), (w1, "w1", None))
                  for half in range(2)]
        FIRST_REUSE = 10
        buffers = [x1, work, heads_out]

        block = ctx.enter_context(nc.Block())

        def settle(engine, settled):
            engine.sem_inc(settled, 1)

        def sweep(engine, body):
            body(-1, False, False, True)
            body(0, False, True, True)
            body(1, True, True, True)
            with engine.Fori(2, BATCH - 1) as t:
                body(t, True, True, True)
            body(BATCH - 1, True, True, False)
            body(BATCH, True, False, False)

        @block.sync
        def _(sp):
            sp.dma_start(bias_q[:], bq).then_inc(small_in, 16)
            sp.dma_start(bias_k[:], bk).then_inc(small_in, 16)
            sp.dma_start(bias_v[:], bv).then_inc(small_in, 16)
            sp.dma_start(out_bias[:], bo.broadcast_to([P, DIM])).then_inc(small_in, 16)
            for c, (src, _, _, half) in enumerate(CHUNKS):
                if c >= 3:
                    sp.wait_ge(w_low, c - 2)
                sp.dma_start(buffers[c % 3][:],
                             src.rearrange("(k p) n -> p k n", p=P)[:, 2 * half:2 * half + 2, :]
                             ).then_inc(chunk_in[c % 3], 16)

            def stack_heads(g, b):
                par = g % 2
                sp.wait_ge(lo["qk"], count(b, 4, g))
                for i in range(GROUP):
                    for j in range(4):
                        first, second = j // 2, 2 + j % 2
                        sp.dma_start(
                            stack[HEAD * j:HEAD * (j + 1), par, i, :, :].bitcast(f32),
                            stage[HEAD * i:HEAD * (i + 1), par, first:second + 1:second - first, :]
                            .bitcast(f32)).then_inc(stacked[par], 16)

            def body(t, prev, cur, nxt):
                p, n = t - 1, t + 1
                if nxt:
                    if started(t):
                        sp.wait_ge(mm["h1"], count(t, 2, 1))
                    sp.dma_start(xa[:], x_v[n, :, :, :]).then_inc(xa_in, 16)
                    if started(t):
                        sp.wait_ge(far_next_ok, count(t, 1, 0))
                    sp.dma_start(adj_in[:], adj_v[n, :, :, :]).then_inc(adj_got, 16)
                if prev:
                    if started(p - 1):
                        sp.wait_ge(keep_ok, count(p - 1, 1, 0))
                    sp.dma_start(adjt_in[:], adjt_v[p, :, :, :]).then_inc(adjt_got, 16)
                if cur:
                    stack_heads(2, t)
                    stack_heads(3, t)
                if nxt:
                    stack_heads(0, n)
                if prev:
                    sp.wait_ge(final, count(p, 2, 1))
                    sp.dma_start(out_v[p, :, :, :], x1[:]).then_inc(stored, 16)
                if nxt:
                    stack_heads(1, n)

            sweep(sp, body)
            sp.wait_ge(stored, 16 * BATCH)

        @block.tensor
        def _(pe):
            def product(dst, parts, tiles):
                last = None
                for k in range(tiles):
                    (aH, bH), (aL, bL) = parts(k)
                    steps = ((aH, bH), (aH, bL), (aL, bH))
                    for s, (a, b) in enumerate(steps):
                        last = nc.tensor.matmul(dst, a, b, start=(k == 0 and s == 0),
                                                stop=(k == tiles - 1 and s == 2))
                return last

            pe.wait_ge(w_low, 4)
            for m in range(KT):
                cols = slice(m * P, (m + 1) * P)
                if m >= RING:
                    pe.wait_ge(merged_lo, m - RING + 1)
                product(ring[m % RING][:],
                        lambda k: ((WH["wo"][:, k, cols], WH["w1"][:, k, :]),
                                   (WL["wo"][:, k, cols], WL["w1"][:, k, :])), KT
                        ).then_inc(merged, 1)
            pe.wait_ge(bv_low, 1)
            pe.wait_ge(w_low, 12)
            pe.wait_ge(merged_lo, 2)
            bvH = eH[:, :, :].rearrange("p a (b m) -> p (a b) m", m=P)
            bvL = eL[:, :, :].rearrange("p a (b m) -> p (a b) m", m=P)
            product(ring[1][:], lambda k: ((bvH[:, k, :], WH["wo"][:, k, :]),
                                           (bvL[:, k, :], WL["wo"][:, k, :])), KT
                    ).then_inc(bias_row, 1)
            pe.wait_ge(bias_ok, 1)
            pe.wait_ge(w_low, len(CHUNKS))
            pe.wait_ge(merged_lo, KT)
            pe.wait_ge(ident_ok, 2)
            pe.wait_ge(ones_ok, 1)

            def scores(u, b):
                g, i = u // GROUP, u % GROUP
                if i == 0:
                    pe.wait_ge(stacked[g % 2], (b * 2 + (g // 2 + 1)) * (16 * 4 * GROUP))
                if u >= 2:
                    pe.wait_ge(masked, count(b, HEADS, u - 2))
                elif started(b - 1):
                    pe.wait_ge(masked, count(b - 1, HEADS, HEADS + u - 2))
                for q in range(QT):
                    last = nc.tensor.matmul(score[u % 2][:, q * NODES:(q + 1) * NODES],
                                            stack[:, g % 2, i, 0, q * P:(q + 1) * P],
                                            stack[:, g % 2, i, 1, :], start=True, stop=True)
                last.then_inc(mm["score"], 1)

            def turn(u, b):
                pe.wait_ge(exped, count(b, HEADS, u))
                if u >= 2:
                    pe.wait_ge(lo["p"], count(b, HEADS, u - 2))
                elif started(b - 1):
                    pe.wait_ge(lo["p"], count(b - 1, HEADS, HEADS + u - 2))
                for q in range(QT):
                    for k in range(QT):
                        at = k * NODES + q * P
                        last = nc.tensor.transpose(turned[u % 2][:, at:at + P],
                                                   probs[:, u % 2, q, k * P:(k + 1) * P], ident[:])
                last.then_inc(mm["turn"], 1)

            def weigh(u, b):
                pe.wait_ge(lo["p"], count(b, HEADS, u))
                if u % (HEADS // 2) == 0:
                    pe.wait_ge(v_low, count(b, 2, u // (HEADS // 2)))
                if u % 2 == 0:
                    if u >= 2:
                        pe.wait_ge(summed, count(b, HEADS // 2, u // 2 - 1))
                    elif started(b - 1):
                        pe.wait_ge(summed, count(b - 1, HEADS // 2, HEADS // 2 - 1))
                for q in range(QT):
                    slot = (u % 2) * QT + q
                    for k in range(QT):
                        cols = slice(q * P, (q + 1) * P)
                        nc.tensor.matmul(pv4[:, slot, 0:VCOLS], pH[:, u % 2, k, cols],
                                         val[:, k, u, 0:VCOLS], start=(k == 0), stop=False)
                        last = nc.tensor.matmul(pv4[:, slot, HEAD:VCOLS], pL[:, u % 2, k, cols],
                                                val[:, k, u, HEAD:VCOLS], start=False,
                                                stop=(k == QT - 1))
                last.then_inc(mm["pv"], 1)

            def dense(name, t, step_t):
                b = t + ROLE[name]
                k = int(name[-1]) if name != "al" else 0
                dst = ring[BANK[name]]
                other, off = bank_before(name, step_t)
                if other is not None:
                    s, per, idx = RELEASE[other]
                    pe.wait_ge(s, count(t + off, per, idx))
                tok = slice(k * P, (k + 1) * P)
                if name.startswith("h1"):
                    pe.wait_ge(normed[0], count(b, 2, k))
                    for d in range(KT):
                        last = nc.tensor.transpose(dst[:, d * P:(d + 1) * P],
                                                   xa[:, k, d * P:(d + 1) * P], ident[:])
                    last.then_inc(mm["h1"], 1)
                elif name.startswith("h2"):
                    pe.wait_ge(normed[1], count(b, 2, k))
                    for d in range(KT):
                        last = nc.tensor.transpose(dst[:, d * P:(d + 1) * P],
                                                   work[:, k, d * P:(d + 1) * P], ident[:])
                    last.then_inc(mm["h2"], 1)
                elif name.startswith("qk"):
                    pe.wait_ge(lo["h1"], count(b, 2, 1))
                    cols = slice(k * P, (k + 1) * P)
                    for half, w in enumerate(("wq", "wk")):
                        last = product(dst[:, half * NODES:(half + 1) * NODES],
                                       lambda d: ((WH[w][:, d, cols], h1H[:, d, :]),
                                                  (WL[w][:, d, cols], h1L[:, d, :])), KT)
                    last.then_inc(mm["qk"], 1)
                elif name.startswith("v"):
                    pe.wait_ge(lo["h1"], count(b, 2, 1))
                    cols = slice(k * NODES, (k + 1) * NODES)
                    for q in range(QT):
                        rows = slice(q * P, (q + 1) * P)
                        last = product(dst[:, q * NODES:(q + 1) * NODES],
                                       lambda d: ((h1H[:, d, rows], WH["wv"][:, d, cols]),
                                                  (h1L[:, d, rows], WL["wv"][:, d, cols])), KT)
                    last.then_inc(mm["v"], 1)
                elif name.startswith("ot"):
                    pe.wait_ge(head_ok, count(b, HEADS // 2, 4 * k + 3))
                    for c in range(2):
                        for q in range(QT):
                            at = c * NODES + q * P
                            last = nc.tensor.transpose(
                                dst[:, at:at + P],
                                heads_out[:, q, (2 * k + c) * P:(2 * k + c + 1) * P], ident[:])
                    last.then_inc(mm["ot"], 1)
                elif name.startswith("wo"):
                    pe.wait_ge(lo["ot"], count(b, 2, 1))
                    product(dst[:], lambda d: ((oH[:, d, tok], WH["wo"][:, d, :]),
                                               (oL[:, d, tok], WL["wo"][:, d, :])), KT
                            ).then_inc(mm["wo"], 1)
                elif name.startswith("hw"):
                    pe.wait_ge(lo["h2"], count(b, 2, k))
                    product(dst[:], lambda d: ((h2H[:, d, tok], WH["w1"][:, d, :]),
                                               (h2L[:, d, tok], WL["w1"][:, d, :])), KT
                            ).then_inc(mm["hw"], 1)
                elif name.startswith("g"):
                    pe.wait_ge(lo["h2"], count(b, 2, 1))
                    for c in range(2):
                        cols = slice((2 * k + c) * P, (2 * k + c + 1) * P)
                        last = product(dst[:, c * NODES:(c + 1) * NODES],
                                       lambda d: ((WH["wm"][:, d, cols], h2H[:, d, :]),
                                                  (WL["wm"][:, d, cols], h2L[:, d, :])), KT)
                    last.then_inc(mm["g"], 1)
                elif name == "al":
                    pe.wait_ge(lo["g"], count(b, 2, 1))
                    for m in range(QT):
                        rows = slice(m * P, (m + 1) * P)
                        last = product(dst[:, m * NODES:(m + 1) * NODES],
                                       lambda d: ((gH[:, d, rows], h2H[:, d, :]),
                                                  (gL[:, d, rows], h2L[:, d, :])), KT)
                    last.then_inc(mm["al"], 1)
                else:
                    pe.wait_ge(lo["e"], count(b, 1, 0))
                    pe.wait_ge(lo["hw"], count(b, 2, 1))
                    product(dst[:], lambda m: ((eH[:, m, tok], hwH[:, m, :]),
                                               (eL[:, m, tok], hwL[:, m, :])), QT
                            ).then_inc(mm["av"], 1)

            def body(t, prev, cur, nxt):
                present = {-1: prev, 0: cur, 1: nxt}
                for s in range(HEADS):
                    if cur and s + 1 < HEADS:
                        scores(s + 1, t)
                    elif nxt and s + 1 == HEADS:
                        scores(0, t + 1)
                    if cur:
                        turn(s, t)
                    if s == 0 and prev:
                        weigh(HEADS - 1, t - 1)
                    elif s > 0 and cur:
                        weigh(s - 1, t)
                    for name in DENSE[s]:
                        if present[ROLE[name]]:
                            dense(name, t, t if isinstance(t, int) else 2)

            for name in ORDER:
                assert len({bank_before(name, t) for t in range(2, BATCH - 1)}) == 1
            sweep(pe, body)

        @block.scalar
        def _(act):
            for c, (_, slot, factor, half) in enumerate(CHUNKS):
                if c == FIRST_REUSE:
                    for m in range(KT):
                        act.wait_ge(merged, m + 1)
                        nc.scalar.activation(WH["wm"][:, m, :], ring[m % RING][:], ACT.Copy
                                             ).then_inc(merged_hi, 1)
                act.wait_ge(chunk_in[c % 3], 16 * (c // 3 + 1))
                nc.scalar.activation(WH[slot][:, 2 * half:2 * half + 2, :], buffers[c % 3][:],
                                     ACT.Copy, scale=factor or 1.0).then_inc(w_high, 1)
            act.wait_ge(bias_q_ok, 1)
            act.wait_ge(small_in, 64)

            def exponentials(u, b):
                act.wait_ge(masked, count(b, HEADS, u))
                for q in range(QT):
                    last = nc.scalar.activation(probs[:, u % 2, q, :], probs[:, u % 2, q, :],
                                                ACT.Exp, bias=least[:, u % 2, q:q + 1], scale=-1.0)
                last.then_inc(exped, 1)

            def turned_high(u, b):
                act.wait_ge(mm["turn"], count(b, HEADS, u))
                if u >= 2:
                    act.wait_ge(mm["pv"], count(b, HEADS, u - 2))
                elif started(b - 1):
                    act.wait_ge(mm["pv"], count(b - 1, HEADS, HEADS + u - 2))
                nc.scalar.activation(pH[:, u % 2, :, :],
                                     turned[u % 2][:].rearrange("p (k n) -> p k n", k=QT),
                                     ACT.Copy).then_inc(hi["p"], 1)

            def values_mid(half, b):
                act.wait_ge(lo["v"], count(b, 2, half))
                rest = v_rest[:].rearrange("p q (h d) -> p q h d", d=HEAD)
                nc.scalar.activation(val[:, :, 8 * half:8 * half + 8, HEAD:2 * HEAD], rest,
                                     ACT.Copy).then_inc(v_mid, 1)

            def dense_high(name, b):
                k = int(name[-1]) if name != "al" else 0
                src = ring[BANK[name]]
                tok = slice(k * P, (k + 1) * P)
                if name.startswith("h1"):
                    act.wait_ge(mm["h1"], count(b, 2, k))
                    if started(b - 1):
                        act.wait_ge(mm["qk"], count(b - 1, 4, 3))
                        act.wait_ge(mm["v"], count(b - 1, 2, 1))
                    nc.scalar.activation(h1H[:, :, tok],
                                         src[:].rearrange("p (d n) -> p d n", d=KT),
                                         ACT.Relu).then_inc(hi["h1"], 1)
                elif name.startswith("h2"):
                    act.wait_ge(mm["h2"], count(b, 2, k))
                    if started(b - 1):
                        act.wait_ge(mm["al"], count(b - 1, 1, 0))
                    nc.scalar.activation(h2H[:, :, tok],
                                         src[:].rearrange("p (d n) -> p d n", d=KT),
                                         ACT.Relu).then_inc(hi["h2"], 1)
                elif name.startswith("qk"):
                    act.wait_ge(mm["qk"], count(b, 4, k))
                    if k >= 2:
                        act.wait_ge(stacked[k % 2], (b * 2 + 1) * (16 * 4 * GROUP))
                    elif started(b - 1):
                        act.wait_ge(stacked[k % 2], b * (2 * 16 * 4 * GROUP))
                    if k >= 2 or started(b - 1):
                        act.wait_ge(mm["score"], count(b, HEADS, GROUP * (k - 1) - 1))
                    nc.scalar.activation(stage[:, k % 2, 0, :], src[:, 0:NODES], ACT.Identity,
                                         bias=bias_q[:, k:k + 1])
                    nc.scalar.activation(stage[:, k % 2, 2, :], src[:, NODES:2 * NODES],
                                         ACT.Identity, bias=bias_k[:, k:k + 1]
                                         ).then_inc(hi["qk"], 1)
                elif name.startswith("v"):
                    act.wait_ge(mm["v"], count(b, 2, k))
                    if started(b - 1):
                        act.wait_ge(mm["pv"], count(b - 1, HEADS, 8 * k + 7))
                    nc.scalar.activation(val[:, :, 8 * k:8 * k + 8, 2 * HEAD:3 * HEAD],
                                         src[:].rearrange("p (q h d) -> p q h d", q=QT, d=HEAD),
                                         ACT.Copy).then_inc(hi["v"], 1)
                elif name.startswith("ot"):
                    act.wait_ge(mm["ot"], count(b, 2, k))
                    if started(b - 1):
                        act.wait_ge(mm["wo"], count(b - 1, 2, 1))
                    nc.scalar.activation(oH[:, 2 * k:2 * k + 2, :],
                                         src[:].rearrange("p (c n) -> p c n", c=2),
                                         ACT.Copy).then_inc(hi["ot"], 1)
                elif name.startswith("hw"):
                    act.wait_ge(mm["hw"], count(b, 2, k))
                    if started(b - 1):
                        act.wait_ge(mm["av"], count(b - 1, 2, 1))
                    nc.scalar.activation(hwH[:, k, :], src[:], ACT.Copy).then_inc(hi["hw"], 1)
                elif name.startswith("g"):
                    act.wait_ge(mm["g"], count(b, 2, k))
                    if started(b - 1):
                        act.wait_ge(mm["al"], count(b - 1, 1, 0))
                    nc.scalar.activation(gH[:, 2 * k:2 * k + 2, :],
                                         src[:].rearrange("p (c n) -> p c n", c=2),
                                         ACT.Copy).then_inc(hi["g"], 1)
                elif name == "al":
                    act.wait_ge(l1_maxed, count(b, 1, 0))
                    for m in range(QT):
                        last = nc.scalar.activation(work[:, 1, m * NODES:(m + 1) * NODES],
                                                    work[:, 0, m * NODES:(m + 1) * NODES], ACT.Exp,
                                                    bias=l1_max[:, m:m + 1],
                                                    accum_out=l1_sum[:, m:m + 1])
                    last.then_inc(l1_exped, 1)
                    act.wait_ge(l1_rcped, count(b, 1, 0))
                    if started(b - 1):
                        act.wait_ge(mm["av"], count(b - 1, 2, 1))
                    for m in range(QT):
                        last = nc.scalar.activation(eH[:, m, :], work[:, 1, m * NODES:(m + 1) * NODES],
                                                    ACT.Copy, scale=l1_rcp[:, m:m + 1])
                    last.then_inc(hi["e"], 1)

            def body(t, prev, cur, nxt):
                p = t - 1
                present = {-1: prev, 0: cur, 1: nxt}
                if prev:
                    if started(p - 1):
                        act.wait_ge(stored, count(p - 1, 16, 15))
                    act.dma_start(x1[:], x_v[p, :, :, :]).then_inc(x1_in, 16)
                for s in range(HEADS):
                    if s == 0 and cur:
                        values_mid(0, t)
                    if s == 1 and cur:
                        values_mid(1, t)
                    if cur:
                        turned_high(s, t)
                    if cur and s + 1 < HEADS:
                        exponentials(s + 1, t)
                    elif nxt and s + 1 == HEADS:
                        exponentials(0, t + 1)
                    for name in DENSE[s]:
                        if present[ROLE[name]]:
                            dense_high(name, t + ROLE[name])

            sweep(act, body)

        @block.vector
        def _(dve):
            dve.wait_ge(small_in, 64)
            nc.vector.tensor_scalar(bias_q[:], bias_q[:], -SCALE, None, ALU.mult
                                    ).then_inc(bias_q_ok, 1)
            bvH = eH[:, :, :].rearrange("p a (b m) -> p (a b) m", m=P)
            bvL = eL[:, :, :].rearrange("p a (b m) -> p (a b) m", m=P)
            bv_all = bias_v[:].unsqueeze(2).broadcast_to([P, KT, P])
            nc.vector.tensor_copy(bvH, bv_all).then_inc(bv_high, 1)
            dve.wait_ge(bv_high, 1)
            nc.vector.tensor_tensor(bvL, bv_all, bvH.bitcast(f32), ALU.subtract).then_inc(bv_low, 1)
            nc.vector.memset(val[:, :, :, 3 * HEAD:VPITCH], 1.0).then_inc(ones_ok, 1)
            for c, (_, slot, factor, half) in enumerate(CHUNKS):
                if c == FIRST_REUSE:
                    for m in range(KT):
                        dve.wait_ge(merged_hi, m + 1)
                        nc.vector.tensor_tensor(WL["wm"][:, m, :], ring[m % RING][:],
                                                WH["wm"][:, m, :].bitcast(f32), ALU.subtract
                                                ).then_inc(merged_lo, 1)
                dve.wait_ge(w_high, c + 1)
                tiles = slice(2 * half, 2 * half + 2)
                nc.vector.scalar_tensor_tensor(out=WL[slot][:, tiles, :], in0=buffers[c % 3][:],
                                               scalar=factor or 1.0,
                                               in1=WH[slot][:, tiles, :].bitcast(f32),
                                               op0=ALU.mult, op1=ALU.subtract).then_inc(w_low, 1)
            dve.wait_ge(bias_row, 1)
            nc.vector.tensor_tensor(out_bias[:], ring[1][:], out_bias[:], ALU.add
                                    ).then_inc(bias_ok, 1)

            def mask(u, b):
                if u == 0:
                    dve.wait_ge(far_ok, count(b, 1, 0))
                dve.wait_ge(mm["score"], count(b, HEADS, u))
                if u >= 2:
                    dve.wait_ge(mm["turn"], count(b, HEADS, u - 2))
                elif started(b - 1):
                    dve.wait_ge(mm["turn"], count(b - 1, HEADS, HEADS + u - 2))
                settle(dve, dve_settled)
                for q in range(QT):
                    last = nc.vector.tensor_tensor_reduce(
                        out=probs[:, u % 2, q, :], in0=score[u % 2][:, q * NODES:(q + 1) * NODES],
                        in1=far[:, q, :], scale=1.0, scalar=FAR, op0=ALU.add, op1=ALU.min,
                        accum_out=least[:, u % 2, q:q + 1])
                last.then_inc(masked, 1)

            def turned_low(u, b):
                dve.wait_ge(hi["p"], count(b, HEADS, u))
                nc.vector.tensor_tensor(pL[:, u % 2, :, :],
                                        turned[u % 2][:].rearrange("p (k n) -> p k n", k=QT),
                                        pH[:, u % 2, :, :], ALU.subtract).then_inc(lo["p"], 1)

            def sum_parts(pair, b):
                dve.wait_ge(mm["pv"], count(b, HEADS, 2 * pair + 1))
                if pair >= 2:
                    dve.wait_ge(head_ok, count(b, HEADS // 2, pair - 2))
                elif started(b - 1):
                    dve.wait_ge(head_ok, count(b - 1, HEADS // 2, HEADS // 2 + pair - 2))
                nc.vector.reciprocal(o_rcp[:, pair % 2, :], pv4[:, :, 3 * HEAD])
                parts = pv4[:, :, 0:3 * HEAD].rearrange("p g (b d) -> p g d b", d=HEAD)
                nc.vector.tensor_reduce(o_sum[:, pair % 2, :, :], parts, AX.X, ALU.add
                                        ).then_inc(summed, 1)

            def norm_stats(which, src, b, ready, per):
                for q in range(QT):
                    dve.wait_ge(ready, count(b, per, q) if per == 2 else count(b, 16, 15))
                    nc.vector.bn_stats(stats[which][:, q, :], src[:, q, :]).then_inc(stat[which], 1)
                for q in range(QT):
                    dve.wait_ge(stat[which], count(b, QT, q))
                    settle(dve, dve_settled)
                    last = nc.vector.bn_aggr(meanvar[which][:, q, :], stats[which][:, q, :])
                last.then_inc(var_ok[which], 1)

            def normalise(which, src, dst, b):
                dve.wait_ge(nstep[which], count(b, NSTEPS, NSTEPS - 1))
                for q in range(QT):
                    nc.vector.tensor_scalar(dst[:, q, :], src[:, q, :], meanvar[which][:, q, 0:1],
                                            rstd[which][:, q:q + 1], ALU.subtract, ALU.mult
                                            ).then_inc(normed[which], 1)

            def relu_low(dst, src, high, done):
                nc.vector.scalar_tensor_tensor(out=dst, in0=src, scalar=0.0,
                                               in1=high.bitcast(f32), op0=ALU.max,
                                               op1=ALU.subtract).then_inc(done, 1)

            def dense_low(name, b):
                k = int(name[-1]) if name != "al" else 0
                src = ring[BANK[name]]
                tok = slice(k * P, (k + 1) * P)
                if name.startswith("h1"):
                    dve.wait_ge(hi["h1"], count(b, 2, k))
                    relu_low(h1L[:, :, tok], src[:].rearrange("p (d n) -> p d n", d=KT),
                             h1H[:, :, tok], lo["h1"])
                elif name.startswith("h2"):
                    dve.wait_ge(hi["h2"], count(b, 2, k))
                    relu_low(h2L[:, :, tok], src[:].rearrange("p (d n) -> p d n", d=KT),
                             h2H[:, :, tok], lo["h2"])
                elif name.startswith("qk"):
                    dve.wait_ge(hi["qk"], count(b, 4, k))
                    nc.vector.scalar_tensor_tensor(
                        out=stage[:, k % 2, 1, :], in0=src[:, 0:NODES], scalar=bias_q[:, k:k + 1],
                        in1=stage[:, k % 2, 0, :].bitcast(f32), op0=ALU.add, op1=ALU.subtract)
                    nc.vector.scalar_tensor_tensor(
                        out=stage[:, k % 2, 3, :], in0=src[:, NODES:2 * NODES],
                        scalar=bias_k[:, k:k + 1], in1=stage[:, k % 2, 2, :].bitcast(f32),
                        op0=ALU.add, op1=ALU.subtract).then_inc(lo["qk"], 1)
                elif name.startswith("v"):
                    dve.wait_ge(hi["v"], count(b, 2, k))
                    if k == 1:
                        dve.wait_ge(v_low, count(b, 2, 0))
                    elif started(b - 1):
                        dve.wait_ge(v_low, count(b - 1, 2, 1))
                    nc.vector.tensor_tensor(
                        v_rest[:].rearrange("p q (h d) -> p q h d", d=HEAD),
                        src[:].rearrange("p (q h d) -> p q h d", q=QT, d=HEAD),
                        val[:, :, 8 * k:8 * k + 8, 2 * HEAD:3 * HEAD], ALU.subtract
                        ).then_inc(lo["v"], 1)
                elif name.startswith("ot"):
                    dve.wait_ge(hi["ot"], count(b, 2, k))
                    nc.vector.tensor_tensor(oL[:, 2 * k:2 * k + 2, :],
                                            src[:].rearrange("p (c n) -> p c n", c=2),
                                            oH[:, 2 * k:2 * k + 2, :].bitcast(f32), ALU.subtract
                                            ).then_inc(lo["ot"], 1)
                elif name.startswith("wo"):
                    dve.wait_ge(mm["wo"], count(b, 2, k))
                    if k == 0:
                        dve.wait_ge(x1_ok, count(b, 1, 0))
                    nc.vector.tensor_tensor(x1[:, k, :], src[:], x1[:, k, :], ALU.add
                                            ).then_inc(added, 1)
                elif name.startswith("hw"):
                    dve.wait_ge(hi["hw"], count(b, 2, k))
                    nc.vector.tensor_tensor(hwL[:, k, :], src[:], hwH[:, k, :].bitcast(f32),
                                            ALU.subtract).then_inc(lo["hw"], 1)
                elif name.startswith("g"):
                    dve.wait_ge(hi["g"], count(b, 2, k))
                    nc.vector.tensor_tensor(gL[:, 2 * k:2 * k + 2, :],
                                            src[:].rearrange("p (c n) -> p c n", c=2),
                                            gH[:, 2 * k:2 * k + 2, :].bitcast(f32), ALU.subtract
                                            ).then_inc(lo["g"], 1)
                elif name == "al":
                    dve.wait_ge(mm["al"], count(b, 1, 0))
                    dve.wait_ge(keep_ok, count(b, 1, 0))
                    nc.vector.scalar_tensor_tensor(
                        out=work[:, 0, :].rearrange("p (m n) -> p m n", m=QT),
                        in0=src[:].rearrange("p (m n) -> p m n", m=QT), scalar=0.0, in1=keep[:],
                        op0=ALU.max, op1=ALU.mult).then_inc(l1_masked, 1)
                    dve.wait_ge(l1_masked, count(b, 1, 0))
                    nc.vector.tensor_reduce(l1_max[:], work[:, 0, :].rearrange(
                        "p (m n) -> p m n", m=QT), AX.X, ALU.max, negate=True).then_inc(l1_maxed, 1)
                    dve.wait_ge(l1_exped, count(b, 1, 0))
                    nc.vector.reciprocal(l1_rcp[:], l1_sum[:]).then_inc(l1_rcped, 1)
                    dve.wait_ge(hi["e"], count(b, 1, 0))
                    for m in range(QT):
                        last = nc.vector.scalar_tensor_tensor(
                            out=eL[:, m, :], in0=work[:, 1, m * NODES:(m + 1) * NODES],
                            scalar=l1_rcp[:, m:m + 1], in1=eH[:, m, :].bitcast(f32),
                            op0=ALU.mult, op1=ALU.subtract)
                    last.then_inc(lo["e"], 1)
                else:
                    dve.wait_ge(mm["av"], count(b, 2, k))
                    nc.vector.tensor_tensor(x1[:, k, :], src[:], x1[:, k, :], ALU.add
                                            ).then_inc(final, 1)

            def body(t, prev, cur, nxt):
                p, n = t - 1, t + 1
                present = {-1: prev, 0: cur, 1: nxt}
                for s in range(HEADS):
                    if cur and s + 1 < HEADS:
                        mask(s + 1, t)
                    elif nxt and s + 1 == HEADS:
                        dve.wait_ge(far_next_ok, count(n, 1, 0))
                        if cur:
                            dve.wait_ge(masked, count(t, HEADS, HEADS - 1))
                        nc.vector.tensor_copy(far[:], far_next[:]).then_inc(far_ok, 1)
                        mask(0, n)
                    if cur:
                        turned_low(s, t)
                    if s == 0 and prev:
                        sum_parts(HEADS // 2 - 1, p)
                    elif s > 0 and s % 2 == 0 and cur:
                        sum_parts(s // 2 - 1, t)
                    if s == 4 and nxt:
                        norm_stats(0, xa, n, xa_in, 1)
                    if s == 5 and prev:
                        normalise(1, x1, work, p)
                    if s == 6 and nxt:
                        normalise(0, xa, xa, n)
                    for name in DENSE[s]:
                        if present[ROLE[name]]:
                            dense_low(name, t + ROLE[name])
                    if s == 3 and prev:
                        norm_stats(1, x1, p, added, 2)

            sweep(dve, body)

        @block.gpsimd
        def _(pool):
            nc.gpsimd.memset(ident[:], 0.0).then_inc(ident_ok, 1)
            pool.wait_ge(ident_ok, 1)
            nc.gpsimd.affine_select(out=ident[:], in_=ident[:], compare_op=ALU.not_equal, fill=1.0,
                                    base=0, pattern=[[-1, P]], channel_multiplier=1
                                    ).then_inc(ident_ok, 1)

            def rsqrt(which, b):
                v, y = newton[which][:, 0, :], rstd[which][:]
                a, c = newton[which][:, 1, :], newton[which][:, 2, :]
                at = [0]

                def step(ins):
                    ins.then_inc(nstep[which], 1)
                    pool.wait_ge(nstep[which], count(b, NSTEPS, at[0]))
                    settle(pool, pool_settled)
                    at[0] += 1

                pool.wait_ge(var_ok[which], count(b, 1, 0))
                settle(pool, pool_settled)
                step(nc.gpsimd.tensor_scalar(v, meanvar[which][:, :, 1], EPS, None, ALU.add))
                step(nc.gpsimd.tensor_scalar(a, v.bitcast(i32), -0.5, float(RSQRT_SEED),
                                             ALU.mult, ALU.add))
                step(nc.gpsimd.tensor_copy(y.bitcast(i32), a))
                for _ in range(NEWTON_ROUNDS):
                    step(nc.gpsimd.tensor_tensor(a, y, y, ALU.mult))
                    step(nc.gpsimd.tensor_tensor(c, a, v, ALU.mult))
                    step(nc.gpsimd.tensor_scalar(a, c, -0.5, 1.5, ALU.mult, ALU.add))
                    step(nc.gpsimd.tensor_tensor(y, y, a, ALU.mult))

            def values_low(half, b):
                pool.wait_ge(v_mid, count(b, 2, half))
                heads = slice(8 * half, 8 * half + 8)
                rest = v_rest[:].rearrange("p q (h d) -> p q h d", d=HEAD)
                for q in range(QT):
                    last = nc.gpsimd.tensor_tensor(val[:, q, heads, 0:HEAD], rest[:, q, :, :],
                                                   val[:, q, heads, HEAD:2 * HEAD], ALU.subtract)
                last.then_inc(v_low, 1)

            def norm_heads(pair, b):
                pool.wait_ge(summed, count(b, HEADS // 2, pair))
                if started(b - 1):
                    pool.wait_ge(mm["ot"], count(b - 1, 2, pair // 4))
                for q in range(QT):
                    at = 2 * pair * HEAD
                    dst = heads_out[:, q, at:at + 2 * HEAD].rearrange("p (h d) -> p h d", h=2)
                    last = nc.gpsimd.tensor_tensor(
                        dst, o_sum[:, pair % 2, q:q + 3:2, :],
                        o_rcp[:, pair % 2, q:q + 3:2].unsqueeze(2).broadcast_to([P, 2, HEAD]),
                        ALU.mult)
                last.then_inc(head_ok, 1)

            def body(t, prev, cur, nxt):
                p, n = t - 1, t + 1
                for s in range(HEADS):
                    if s == 0 and cur:
                        values_low(0, t)
                    if s == 0 and prev:
                        norm_heads(HEADS // 2 - 1, p)
                    elif s > 0 and s % 2 == 0 and cur:
                        norm_heads(s // 2 - 1, t)
                    if s == 1 and cur:
                        values_low(1, t)
                    if s == 1 and prev:
                        pool.wait_ge(x1_in, count(p, 16, 15))
                        for q in range(QT):
                            last = nc.gpsimd.tensor_tensor(x1[:, q, :], x1[:, q, :], out_bias[:],
                                                           ALU.add)
                        last.then_inc(x1_ok, 1)
                    if s == 4 and prev:
                        rsqrt(1, p)
                    if s == 5 and nxt:
                        rsqrt(0, n)
                    if s == 6 and prev:
                        pool.wait_ge(adjt_got, count(p, 16, 15))
                        if started(p - 1):
                            pool.wait_ge(l1_masked, count(p - 1, 1, 0))
                        settle(pool, pool_settled)
                        for q in range(QT):
                            last = nc.gpsimd.tensor_scalar(keep[:, q, :], adjt_in[:, q, :], 0, 0,
                                                           ALU.is_equal, ALU.is_equal)
                        last.then_inc(keep_ok, 1)
                    if s == 8 and nxt:
                        pool.wait_ge(adj_got, count(n, 16, 15))
                        if started(t):
                            pool.wait_ge(far_ok, count(t, 1, 0))
                        settle(pool, pool_settled)
                        for q in range(QT):
                            last = nc.gpsimd.tensor_scalar(far_next[:, q, :], adj_in[:, q, :], 0,
                                                           FAR, ALU.is_equal, ALU.mult)
                        last.then_inc(far_next_ok, 1)

            sweep(pool, body)


def kernel(**inputs):
    import numpy as np
    import concourse.bacc as bacc
    from concourse.bass_utils import run_bass_kernel_spmd

    def columns(v):
        return np.ascontiguousarray(np.asarray(v).reshape(KT, P).T)

    src = {k: np.asarray(v) for k, v in inputs.items()}
    arrays = {
        "x": src["x"],
        "adj": src["adj"],
        "adj_t": np.ascontiguousarray(src["adj"].transpose(0, 2, 1)),
        "wq": src["L0_gnn_Wq"], "wk": src["L0_gnn_Wk"], "wv": src["L0_gnn_Wv"],
        "wo": src["L0_gnn_Wo"],
        "bq": columns(src["L0_gnn_bq"]), "bk": columns(src["L0_gnn_bk"]),
        "bv": columns(src["L0_gnn_bv"]), "bo": src["L0_gnn_bo"].reshape(1, DIM),
        "w1": src["L1_gnn_weight"],
        "wq1_t": np.ascontiguousarray(src["L1_gnn_wq"].T),
        "wk1_t": np.ascontiguousarray(src["L1_gnn_wk"].T),
    }
    nc = bacc.Bacc("TRN2", target_bir_lowering=False, num_devices=1)
    args = {n: nc.dram_tensor(f"{n}_dram", a.shape, mybir.dt.from_np(a.dtype),
                              kind="ExternalInput").ap() for n, a in arrays.items()}
    out = nc.dram_tensor("out_dram", (BATCH, NODES, DIM), mybir.dt.float32,
                         kind="ExternalOutput").ap()
    two_layers(nc, **args, out=out)
    r = run_bass_kernel_spmd(nc, [{f"{n}_dram": a for n, a in arrays.items()}], core_ids=[0])
    return r.results[0]["out_dram"]
```

```python
import concourse.bass as bass
from concourse import mybir
from contextlib import ExitStack

BATCH, NODES, DIM, HEADS = 32, 256, 512, 16
HEAD = DIM // HEADS
P = 128
KT = DIM // P
QT = NODES // P
GROUP = P // HEAD
VCOLS = 3 * HEAD + 1
VPITCH = VCOLS + 1
SCALE = HEAD ** -0.5
EPS = 1e-5
FAR = 3.0e38
RSQRT_SEED = 0x5F3759DF
NEWTON_ROUNDS = 3
NSTEPS = 2 + 3 * NEWTON_ROUNDS

DENSE = [
    ["v1"],
    ["qk2", "ot1"],
    ["wo0"],
    ["wo1"],
    [],
    ["qk3", "h2_0", "h2_1"],
    ["hw0", "h1_0", "h1_1"],
    ["g0"],
    ["g1"],
    ["qk0"],
    ["al"],
    ["hw1"],
    ["v0"],
    ["av0", "av1"],
    ["qk1"],
    ["ot0"],
]
RING = 3
AHEAD = 2
ORDER = [name for step in DENSE for name in step]
assert len(ORDER) % RING == 0 and len(DENSE) == HEADS
ROLE = {"v1": 0, "ot1": -1, "qk2": 0, "wo0": -1, "wo1": -1, "qk3": 0, "h2_0": -1, "h2_1": -1,
        "hw0": -1, "g0": -1, "g1": -1, "h1_0": 1, "h1_1": 1, "hw1": -1, "qk0": 1, "al": -1,
        "av0": -1, "av1": -1, "qk1": 1, "ot0": 0, "v0": 1}
AL_STEP = next(s for s, names in enumerate(DENSE) if "al" in names)
MID = (next(s for s, names in enumerate(DENSE) if "v0" in names) + 1, 2)
STATS1, NORM1 = 8, 11
VAR2, NORM2 = 4, 5
X1_STEP, KEEP_STEP, FAR_STEP = 1, 6, 8
BANK = {name: i % RING for i, name in enumerate(ORDER)}


def count(graph, per_graph, k):
    return graph * per_graph + (k + 1)


def started(graph):
    return not (isinstance(graph, int) and graph < 0)


def bank_before(name, t):
    at, shift = ORDER.index(name), 0
    while True:
        at -= RING
        if at < 0:
            at, shift = at + len(ORDER), shift - 1
        other = ORDER[at]
        graph = t + shift + ROLE[other]
        if t + shift < -1:
            return None, 0
        if 0 <= graph < BATCH:
            return other, graph - t


def two_layers(nc, x, adj, adj_t, wq, wk, wv, wo, bq, bk, bv, bo, w1, wq1_t, wk1_t, out):
    f32, f32r = mybir.dt.float32, mybir.dt.float32r
    bf16, f16, i32 = mybir.dt.bfloat16, mybir.dt.float16, mybir.dt.int32
    ALU, ACT, AX = mybir.AluOpType, mybir.ActivationFunctionType, mybir.AxisListType

    x_v = x.rearrange("b (q p) d -> b p q d", p=P)
    out_v = out.rearrange("b (q p) d -> b p q d", p=P)
    adj_v = adj.rearrange("b (q p) k -> b p q k", p=P)
    adjt_v = adj_t.rearrange("b (q p) k -> b p q k", p=P)

    ctx = ExitStack()
    with ctx:
        def sb(name, shape, dt):
            return ctx.enter_context(nc.sbuf_tensor(name, shape, dt))

        def bank(name):
            return ctx.enter_context(nc.psum_tensor(name, [P, 512], f32))

        def sem(name):
            return ctx.enter_context(nc.semaphore(name))

        WH = {n: sb(f"{n}_hi", [P, KT, DIM], f32r) for n in ("wq", "wk", "wv", "wo", "wm", "w1")}
        WL = {n: sb(f"{n}_lo", [P, KT, DIM], f32r) for n in ("wq", "wk", "wv", "wo", "wm", "w1")}
        ident = sb("ident", [P, P], f32)
        bias_q = sb("bias_q", [P, KT], f32)
        bias_k = sb("bias_k", [P, KT], f32)
        bias_v = sb("bias_v", [P, KT], f32)
        out_bias = sb("out_bias", [P, DIM], f32)

        xa = sb("xa", [P, QT, DIM], f32)
        x1 = sb("x1", [P, QT, DIM], f32)
        adj_in = sb("adj_in", [P, QT, NODES], i32)
        adjt_in = sb("adjt_in", [P, QT, NODES], i32)
        far_next = sb("far_next", [P, QT, NODES], bf16)
        far = sb("far", [P, QT, NODES], bf16)
        keep = sb("keep", [P, QT, NODES], bf16)
        h1H = sb("h1_hi", [P, KT, NODES], f32r)
        h1L = sb("h1_lo", [P, KT, NODES], f32r)
        stage = sb("stage", [P, 2, 4, NODES], f32r)
        stack = sb("stack", [P, 2, GROUP, 2, NODES], f32r)
        val = sb("val", [P, QT, HEADS, VPITCH], bf16)
        v_rest = sb("v_rest", [P, QT, NODES], f32)
        probs = sb("probs", [P, 2, QT, NODES], f32)
        least = sb("least", [P, 2, QT], f32)
        pH = sb("probs_t_hi", [P, 2, QT, NODES], f16)
        pL = sb("probs_t_lo", [P, 2, QT, NODES], f16)
        o_sum = sb("o_sum", [P, 2, 4, HEAD], f32)
        o_rcp = sb("o_rcp", [P, 2, 4], f32)
        heads_out = sb("heads_out", [P, QT, DIM], f32)
        oH = sb("heads_t_hi", [P, KT, NODES], f32r)
        oL = sb("heads_t_lo", [P, KT, NODES], f32r)
        work = sb("work", [P, QT, DIM], f32)
        h2H = sb("h2_hi", [P, KT, NODES], f32r)
        h2L = sb("h2_lo", [P, KT, NODES], f32r)
        gH = sb("g_hi", [P, KT, NODES], f32r)
        gL = sb("g_lo", [P, KT, NODES], f32r)
        hwH = sb("hw_hi", [P, QT, DIM], f32r)
        hwL = sb("hw_lo", [P, QT, DIM], f32r)
        eH = sb("e_hi", [P, QT, NODES], f32r)
        eL = sb("e_lo", [P, QT, NODES], f32r)
        l1_max = sb("l1_max", [P, QT], f32)
        l1_sum = sb("l1_sum", [P, QT], f32)
        l1_rcp = sb("l1_rcp", [P, QT], f32)
        stats = [sb(f"stats{n}", [P, QT, 6], f32) for n in (1, 2)]
        meanvar = [sb(f"meanvar{n}", [P, QT, 2], f32) for n in (1, 2)]
        rstd = [sb(f"rstd{n}", [P, QT], f32) for n in (1, 2)]
        newton = [sb(f"newton{n}", [P, 3, QT], f32) for n in (1, 2)]

        score = [bank("score0"), bank("score1")]
        turned = [bank("turned0"), bank("turned1")]
        pv = bank("pv")
        ring = [bank(f"ring{i}") for i in range(RING)]
        pv4 = pv[:, 0:4 * VPITCH].rearrange("p (g c) -> p g c", c=VPITCH)

        xa_in, x1_in = sem("xa_in"), sem("x1_in")
        adj_got, adjt_got = sem("adj_got"), sem("adjt_got")
        stacked = [[sem(f"stacked{par}{i}") for i in range(GROUP)] for par in range(2)]
        stored = sem("stored")
        small_in = sem("small_in")
        chunk_in = [sem(f"chunk_in{i}") for i in range(3)]
        ident_ok, ones_ok = sem("ident_ok"), sem("ones_ok")
        w_high, w_low = sem("w_high"), sem("w_low")
        bv_high, bv_low = sem("bv_high"), sem("bv_low")
        bias_row, merged = sem("bias_row"), sem("merged")
        merged_hi, merged_lo = sem("merged_hi"), sem("merged_lo")
        bias_q_ok, bias_ok = sem("bias_q_ok"), sem("bias_ok")
        mm = {n: sem(f"mm_{n}") for n in
              ("h1", "qk", "v", "score", "turn", "pv", "ot", "wo", "h2", "g", "al", "hw", "av")}
        hi = {n: sem(f"hi_{n}") for n in ("h1", "qk", "v", "p", "ot", "h2", "g", "e", "hw")}
        v_mid, exped, l1_exped = sem("v_mid"), sem("exped"), sem("l1_exped")
        lo = {n: sem(f"lo_{n}") for n in ("h1", "qk", "v", "p", "ot", "h2", "g", "e", "hw")}
        masked, summed = sem("masked"), sem("summed")
        added, l1_masked, l1_maxed, l1_rcped, final = (
            sem("added"), sem("l1_masked"), sem("l1_maxed"), sem("l1_rcped"), sem("final"))
        stat = [sem("stat1"), sem("stat2")]
        var_ok = [sem("var_ok1"), sem("var_ok2")]
        normed = [sem("normed1"), sem("normed2")]
        far_ok = sem("far_ok")
        v_low, head_ok = sem("v_low"), sem("head_ok")
        nstep = [sem("nstep1"), sem("nstep2")]
        dve_settled, pool_settled = sem("dve_settled"), sem("pool_settled")
        x1_ok, keep_ok, far_next_ok = sem("x1_ok"), sem("keep_ok"), sem("far_next_ok")

        RELEASE = {"v1": (lo["v"], 2, 1), "v0": (lo["v"], 2, 0),
                   "ot0": (lo["ot"], 2, 0), "ot1": (lo["ot"], 2, 1),
                   "wo0": (added, 2, 0), "wo1": (added, 2, 1),
                   "h1_0": (lo["h1"], 2, 0), "h1_1": (lo["h1"], 2, 1),
                   "h2_0": (lo["h2"], 2, 0), "h2_1": (lo["h2"], 2, 1),
                   "g0": (lo["g"], 2, 0), "g1": (lo["g"], 2, 1), "al": (l1_masked, 1, 0),
                   "hw0": (lo["hw"], 2, 0), "hw1": (lo["hw"], 2, 1),
                   "av0": (final, 2, 0), "av1": (final, 2, 1),
                   "qk0": (lo["qk"], 4, 0), "qk1": (lo["qk"], 4, 1),
                   "qk2": (lo["qk"], 4, 2), "qk3": (lo["qk"], 4, 3)}

        CHUNKS = [(src, slot, factor, half)
                  for src, slot, factor in ((wk1_t, "wo", None), (wq1_t, "w1", None),
                                            (wq, "wq", -SCALE), (wk, "wk", None), (wv, "wv", None),
                                            (wo, "wo", None), (w1, "w1", None))
                  for half in range(2)]
        FIRST_REUSE = 10
        buffers = [x1, work, heads_out]

        block = ctx.enter_context(nc.Block())

        def settle(engine, settled):
            engine.sem_inc(settled, 1)

        def sweep(engine, body):
            body(-1, False, False, True, True)
            body(0, False, True, True, True)
            body(1, True, True, True, True)
            with engine.Fori(2, BATCH - 2) as t:
                body(t, True, True, True, True)
            body(BATCH - 2, True, True, True, False)
            body(BATCH - 1, True, True, False, False)
            body(BATCH, True, False, False, False)

        @block.sync
        def _(sp):
            sp.dma_start(bias_q[:], bq).then_inc(small_in, 16)
            sp.dma_start(bias_k[:], bk).then_inc(small_in, 16)
            sp.dma_start(bias_v[:], bv).then_inc(small_in, 16)
            sp.dma_start(out_bias[:], bo.broadcast_to([P, DIM])).then_inc(small_in, 16)
            for c, (src, _, _, half) in enumerate(CHUNKS):
                if c >= 3:
                    sp.wait_ge(w_low, c - 2)
                sp.dma_start(buffers[c % 3][:],
                             src.rearrange("(k p) n -> p k n", p=P)[:, 2 * half:2 * half + 2, :]
                             ).then_inc(chunk_in[c % 3], 16)

            def stack_heads(g, b):
                par = g % 2
                sp.wait_ge(lo["qk"], count(b, 4, g))
                for i in range(GROUP):
                    for j in range(4):
                        first, second = j // 2, 2 + j % 2
                        sp.dma_start(
                            stack[HEAD * j:HEAD * (j + 1), par, i, :, :].bitcast(f32),
                            stage[HEAD * i:HEAD * (i + 1), par, first:second + 1:second - first, :]
                            .bitcast(f32)).then_inc(stacked[par][i], 16)

            def body(t, prev, cur, nxt, later):
                p, n = t - 1, t + 1
                if nxt:
                    if started(t):
                        sp.wait_ge(far_next_ok, count(t, 1, 0))
                    sp.dma_start(adj_in[:], adj_v[n, :, :, :]).then_inc(adj_got, 16)
                if prev:
                    if started(p - 1):
                        sp.wait_ge(keep_ok, count(p - 1, 1, 0))
                    sp.dma_start(adjt_in[:], adjt_v[p, :, :, :]).then_inc(adjt_got, 16)
                if cur:
                    stack_heads(1, t)
                    stack_heads(2, t)
                if later:
                    sp.wait_ge(mm["h1"], count(n, 2, 1))
                    sp.dma_start(xa[:], x_v[n + 1, :, :, :]).then_inc(xa_in, 16)
                if cur:
                    stack_heads(3, t)
                if nxt:
                    stack_heads(0, n)
                if prev:
                    sp.wait_ge(final, count(p, 2, 1))
                    sp.dma_start(out_v[p, :, :, :], x1[:]).then_inc(stored, 16)

            sp.dma_start(xa[:], x_v[0, :, :, :]).then_inc(xa_in, 16)
            sweep(sp, body)
            sp.wait_ge(stored, 16 * BATCH)

        @block.tensor
        def _(pe):
            def product(dst, parts, tiles):
                last = None
                for k in range(tiles):
                    (aH, bH), (aL, bL) = parts(k)
                    steps = ((aH, bH), (aH, bL), (aL, bH))
                    for s, (a, b) in enumerate(steps):
                        last = nc.tensor.matmul(dst, a, b, start=(k == 0 and s == 0),
                                                stop=(k == tiles - 1 and s == 2))
                return last

            pe.wait_ge(w_low, 4)
            for m in range(KT):
                cols = slice(m * P, (m + 1) * P)
                if m >= RING:
                    pe.wait_ge(merged_lo, m - RING + 1)
                product(ring[m % RING][:],
                        lambda k: ((WH["wo"][:, k, cols], WH["w1"][:, k, :]),
                                   (WL["wo"][:, k, cols], WL["w1"][:, k, :])), KT
                        ).then_inc(merged, 1)
            pe.wait_ge(bv_low, 1)
            pe.wait_ge(w_low, 12)
            pe.wait_ge(merged_lo, 2)
            bvH = eH[:, :, :].rearrange("p a (b m) -> p (a b) m", m=P)
            bvL = eL[:, :, :].rearrange("p a (b m) -> p (a b) m", m=P)
            product(ring[1][:], lambda k: ((bvH[:, k, :], WH["wo"][:, k, :]),
                                           (bvL[:, k, :], WL["wo"][:, k, :])), KT
                    ).then_inc(bias_row, 1)
            pe.wait_ge(bias_ok, 1)
            pe.wait_ge(w_low, len(CHUNKS))
            pe.wait_ge(merged_lo, KT)
            pe.wait_ge(ident_ok, 2)
            pe.wait_ge(ones_ok, 1)

            def scores(u, b):
                g, i = u // GROUP, u % GROUP
                pe.wait_ge(stacked[g % 2][i], count(b, 2, g // 2) * (16 * 4))
                if u >= 2:
                    pe.wait_ge(masked, count(b, HEADS, u - 2))
                elif started(b - 1):
                    pe.wait_ge(masked, count(b - 1, HEADS, HEADS + u - 2))
                for q in range(QT):
                    last = nc.tensor.matmul(score[u % 2][:, q * NODES:(q + 1) * NODES],
                                            stack[:, g % 2, i, 0, q * P:(q + 1) * P],
                                            stack[:, g % 2, i, 1, :], start=True, stop=True)
                last.then_inc(mm["score"], 1)

            def turn(u, b):
                pe.wait_ge(exped, count(b, HEADS, u))
                if u >= 2:
                    pe.wait_ge(lo["p"], count(b, HEADS, u - 2))
                elif started(b - 1):
                    pe.wait_ge(lo["p"], count(b - 1, HEADS, HEADS + u - 2))
                for q in range(QT):
                    for k in range(QT):
                        at = k * NODES + q * P
                        last = nc.tensor.transpose(turned[u % 2][:, at:at + P],
                                                   probs[:, u % 2, q, k * P:(k + 1) * P], ident[:])
                last.then_inc(mm["turn"], 1)

            def weigh(u, b):
                pe.wait_ge(lo["p"], count(b, HEADS, u))
                if u % (HEADS // 2) == 0:
                    pe.wait_ge(v_low, count(b, 2, u // (HEADS // 2)))
                if u % 2 == 0:
                    if u >= 2:
                        pe.wait_ge(summed, count(b, HEADS // 2, u // 2 - 1))
                    elif started(b - 1):
                        pe.wait_ge(summed, count(b - 1, HEADS // 2, HEADS // 2 - 1))
                for q in range(QT):
                    slot = (u % 2) * QT + q
                    for k in range(QT):
                        cols = slice(q * P, (q + 1) * P)
                        nc.tensor.matmul(pv4[:, slot, 0:VCOLS], pH[:, u % 2, k, cols],
                                         val[:, k, u, 0:VCOLS], start=(k == 0), stop=False)
                        last = nc.tensor.matmul(pv4[:, slot, HEAD:VCOLS], pL[:, u % 2, k, cols],
                                                val[:, k, u, HEAD:VCOLS], start=False,
                                                stop=(k == QT - 1))
                last.then_inc(mm["pv"], 1)

            def dense(name, t, step_t):
                b = t + ROLE[name]
                k = int(name[-1]) if name != "al" else 0
                dst = ring[BANK[name]]
                other, off = bank_before(name, step_t)
                if other is not None:
                    s, per, idx = RELEASE[other]
                    pe.wait_ge(s, count(t + off, per, idx))
                tok = slice(k * P, (k + 1) * P)
                if name.startswith("h1"):
                    pe.wait_ge(normed[0], count(b, 2, k))
                    for d in range(KT):
                        last = nc.tensor.transpose(dst[:, d * P:(d + 1) * P],
                                                   xa[:, k, d * P:(d + 1) * P], ident[:])
                    last.then_inc(mm["h1"], 1)
                elif name.startswith("h2"):
                    pe.wait_ge(normed[1], count(b, 2, k))
                    for d in range(KT):
                        last = nc.tensor.transpose(dst[:, d * P:(d + 1) * P],
                                                   work[:, k, d * P:(d + 1) * P], ident[:])
                    last.then_inc(mm["h2"], 1)
                elif name.startswith("qk"):
                    pe.wait_ge(lo["h1"], count(b, 2, 1))
                    cols = slice(k * P, (k + 1) * P)
                    for half, w in enumerate(("wq", "wk")):
                        last = product(dst[:, half * NODES:(half + 1) * NODES],
                                       lambda d: ((WH[w][:, d, cols], h1H[:, d, :]),
                                                  (WL[w][:, d, cols], h1L[:, d, :])), KT)
                    last.then_inc(mm["qk"], 1)
                elif name.startswith("v"):
                    pe.wait_ge(lo["h1"], count(b, 2, 1))
                    cols = slice(k * NODES, (k + 1) * NODES)
                    for q in range(QT):
                        rows = slice(q * P, (q + 1) * P)
                        last = product(dst[:, q * NODES:(q + 1) * NODES],
                                       lambda d: ((h1H[:, d, rows], WH["wv"][:, d, cols]),
                                                  (h1L[:, d, rows], WL["wv"][:, d, cols])), KT)
                    last.then_inc(mm["v"], 1)
                elif name.startswith("ot"):
                    pe.wait_ge(head_ok, count(b, HEADS // 2, 4 * k + 3))
                    for c in range(2):
                        for q in range(QT):
                            at = c * NODES + q * P
                            last = nc.tensor.transpose(
                                dst[:, at:at + P],
                                heads_out[:, q, (2 * k + c) * P:(2 * k + c + 1) * P], ident[:])
                    last.then_inc(mm["ot"], 1)
                elif name.startswith("wo"):
                    pe.wait_ge(lo["ot"], count(b, 2, 1))
                    product(dst[:], lambda d: ((oH[:, d, tok], WH["wo"][:, d, :]),
                                               (oL[:, d, tok], WL["wo"][:, d, :])), KT
                            ).then_inc(mm["wo"], 1)
                elif name.startswith("hw"):
                    pe.wait_ge(lo["h2"], count(b, 2, k))
                    product(dst[:], lambda d: ((h2H[:, d, tok], WH["w1"][:, d, :]),
                                               (h2L[:, d, tok], WL["w1"][:, d, :])), KT
                            ).then_inc(mm["hw"], 1)
                elif name.startswith("g"):
                    pe.wait_ge(lo["h2"], count(b, 2, 1))
                    for c in range(2):
                        cols = slice((2 * k + c) * P, (2 * k + c + 1) * P)
                        last = product(dst[:, c * NODES:(c + 1) * NODES],
                                       lambda d: ((WH["wm"][:, d, cols], h2H[:, d, :]),
                                                  (WL["wm"][:, d, cols], h2L[:, d, :])), KT)
                    last.then_inc(mm["g"], 1)
                elif name == "al":
                    pe.wait_ge(lo["g"], count(b, 2, 1))
                    for m in range(QT):
                        rows = slice(m * P, (m + 1) * P)
                        last = product(dst[:, m * NODES:(m + 1) * NODES],
                                       lambda d: ((gH[:, d, rows], h2H[:, d, :]),
                                                  (gL[:, d, rows], h2L[:, d, :])), KT)
                    last.then_inc(mm["al"], 1)
                else:
                    pe.wait_ge(lo["e"], count(b, 1, 0))
                    pe.wait_ge(lo["hw"], count(b, 2, 1))
                    product(dst[:], lambda m: ((eH[:, m, tok], hwH[:, m, :]),
                                               (eL[:, m, tok], hwL[:, m, :])), QT
                            ).then_inc(mm["av"], 1)

            def body(t, prev, cur, nxt, later):
                present = {-1: prev, 0: cur, 1: nxt}
                for s in range(HEADS):
                    if cur and s + AHEAD < HEADS:
                        scores(s + AHEAD, t)
                    elif nxt and s + AHEAD >= HEADS:
                        scores(s + AHEAD - HEADS, t + 1)
                    if cur:
                        turn(s, t)
                    if s == 0 and prev:
                        weigh(HEADS - 1, t - 1)
                    elif s > 0 and cur:
                        weigh(s - 1, t)
                    for name in DENSE[s]:
                        if present[ROLE[name]]:
                            dense(name, t, t if isinstance(t, int) else 2)

            for name in ORDER:
                assert len({bank_before(name, t) for t in range(2, BATCH - 2)}) == 1
            sweep(pe, body)

        @block.scalar
        def _(act):
            for c, (_, slot, factor, half) in enumerate(CHUNKS):
                if c == FIRST_REUSE:
                    for m in range(KT):
                        act.wait_ge(merged, m + 1)
                        nc.scalar.activation(WH["wm"][:, m, :], ring[m % RING][:], ACT.Copy
                                             ).then_inc(merged_hi, 1)
                act.wait_ge(chunk_in[c % 3], 16 * (c // 3 + 1))
                nc.scalar.activation(WH[slot][:, 2 * half:2 * half + 2, :], buffers[c % 3][:],
                                     ACT.Copy, scale=factor or 1.0).then_inc(w_high, 1)
            act.wait_ge(bias_q_ok, 1)
            act.wait_ge(small_in, 64)

            def exponentials(u, b):
                act.wait_ge(masked, count(b, HEADS, u))
                for q in range(QT):
                    last = nc.scalar.activation(probs[:, u % 2, q, :], probs[:, u % 2, q, :],
                                                ACT.Exp, bias=least[:, u % 2, q:q + 1], scale=-1.0)
                last.then_inc(exped, 1)

            def turned_high(u, b):
                act.wait_ge(mm["turn"], count(b, HEADS, u))
                if u >= 2:
                    act.wait_ge(mm["pv"], count(b, HEADS, u - 2))
                elif started(b - 1):
                    act.wait_ge(mm["pv"], count(b - 1, HEADS, HEADS + u - 2))
                nc.scalar.activation(pH[:, u % 2, :, :],
                                     turned[u % 2][:].rearrange("p (k n) -> p k n", k=QT),
                                     ACT.Copy).then_inc(hi["p"], 1)

            def values_mid(half, b):
                act.wait_ge(lo["v"], count(b, 2, half))
                rest = v_rest[:].rearrange("p q (h d) -> p q h d", d=HEAD)
                nc.scalar.activation(val[:, :, 8 * half:8 * half + 8, HEAD:2 * HEAD], rest,
                                     ACT.Copy).then_inc(v_mid, 1)

            def dense_high(name, b):
                k = int(name[-1]) if name != "al" else 0
                src = ring[BANK[name]]
                tok = slice(k * P, (k + 1) * P)
                if name.startswith("h1"):
                    act.wait_ge(mm["h1"], count(b, 2, k))
                    if started(b - 1):
                        act.wait_ge(mm["qk"], count(b - 1, 4, 3))
                        act.wait_ge(mm["v"], count(b - 1, 2, 1))
                    nc.scalar.activation(h1H[:, :, tok],
                                         src[:].rearrange("p (d n) -> p d n", d=KT),
                                         ACT.Relu).then_inc(hi["h1"], 1)
                elif name.startswith("h2"):
                    act.wait_ge(mm["h2"], count(b, 2, k))
                    if started(b - 1):
                        act.wait_ge(mm["al"], count(b - 1, 1, 0))
                    nc.scalar.activation(h2H[:, :, tok],
                                         src[:].rearrange("p (d n) -> p d n", d=KT),
                                         ACT.Relu).then_inc(hi["h2"], 1)
                elif name.startswith("qk"):
                    act.wait_ge(mm["qk"], count(b, 4, k))
                    if k >= 2 or started(b - 1):
                        act.wait_ge(mm["score"], count(b, HEADS, GROUP * (k - 1) - 1))
                    nc.scalar.activation(stage[:, k % 2, 0, :], src[:, 0:NODES], ACT.Identity,
                                         bias=bias_q[:, k:k + 1])
                    nc.scalar.activation(stage[:, k % 2, 2, :], src[:, NODES:2 * NODES],
                                         ACT.Identity, bias=bias_k[:, k:k + 1]
                                         ).then_inc(hi["qk"], 1)
                elif name.startswith("v"):
                    act.wait_ge(mm["v"], count(b, 2, k))
                    if started(b - 1):
                        act.wait_ge(mm["pv"], count(b - 1, HEADS, 8 * k + 7))
                    nc.scalar.activation(val[:, :, 8 * k:8 * k + 8, 2 * HEAD:3 * HEAD],
                                         src[:].rearrange("p (q h d) -> p q h d", q=QT, d=HEAD),
                                         ACT.Copy).then_inc(hi["v"], 1)
                elif name.startswith("ot"):
                    act.wait_ge(mm["ot"], count(b, 2, k))
                    if started(b - 1):
                        act.wait_ge(mm["wo"], count(b - 1, 2, 1))
                    nc.scalar.activation(oH[:, 2 * k:2 * k + 2, :],
                                         src[:].rearrange("p (c n) -> p c n", c=2),
                                         ACT.Copy).then_inc(hi["ot"], 1)
                elif name.startswith("hw"):
                    act.wait_ge(mm["hw"], count(b, 2, k))
                    if started(b - 1):
                        act.wait_ge(mm["av"], count(b - 1, 2, 1))
                    nc.scalar.activation(hwH[:, k, :], src[:], ACT.Copy).then_inc(hi["hw"], 1)
                elif name.startswith("g"):
                    act.wait_ge(mm["g"], count(b, 2, k))
                    if started(b - 1):
                        act.wait_ge(mm["al"], count(b - 1, 1, 0))
                    nc.scalar.activation(gH[:, 2 * k:2 * k + 2, :],
                                         src[:].rearrange("p (c n) -> p c n", c=2),
                                         ACT.Copy).then_inc(hi["g"], 1)

            def second_softmax(s, b):
                if s == AL_STEP + 1:
                    act.wait_ge(l1_maxed, count(b, 1, 0))
                    for m in range(QT):
                        last = nc.scalar.activation(work[:, 1, m * NODES:(m + 1) * NODES],
                                                    work[:, 0, m * NODES:(m + 1) * NODES], ACT.Exp,
                                                    bias=l1_max[:, m:m + 1],
                                                    accum_out=l1_sum[:, m:m + 1])
                    last.then_inc(l1_exped, 1)
                if s == AL_STEP + 2:
                    act.wait_ge(l1_rcped, count(b, 1, 0))
                    if started(b - 1):
                        act.wait_ge(mm["av"], count(b - 1, 2, 1))
                    for m in range(QT):
                        last = nc.scalar.activation(eH[:, m, :], work[:, 1, m * NODES:(m + 1) * NODES],
                                                    ACT.Copy, scale=l1_rcp[:, m:m + 1])
                    last.then_inc(hi["e"], 1)

            def body(t, prev, cur, nxt, later):
                p, n = t - 1, t + 1
                present = {-1: prev, 0: cur, 1: nxt}
                if prev:
                    if started(p - 1):
                        act.wait_ge(stored, count(p - 1, 16, 15))
                    act.dma_start(x1[:], x_v[p, :, :, :]).then_inc(x1_in, 16)
                for s in range(HEADS):
                    if cur:
                        turned_high(s, t)
                    if cur and s + 1 < HEADS:
                        exponentials(s + 1, t)
                    elif nxt and s + 1 == HEADS:
                        exponentials(0, t + 1)
                    if s == MID[0] and nxt:
                        values_mid(0, n)
                    if s == MID[1] and cur:
                        values_mid(1, t)
                    if prev:
                        second_softmax(s, p)
                    for name in DENSE[s]:
                        if present[ROLE[name]]:
                            dense_high(name, t + ROLE[name])

            sweep(act, body)

        @block.vector
        def _(dve):
            dve.wait_ge(small_in, 64)
            nc.vector.tensor_scalar(bias_q[:], bias_q[:], -SCALE, None, ALU.mult
                                    ).then_inc(bias_q_ok, 1)
            bvH = eH[:, :, :].rearrange("p a (b m) -> p (a b) m", m=P)
            bvL = eL[:, :, :].rearrange("p a (b m) -> p (a b) m", m=P)
            bv_all = bias_v[:].unsqueeze(2).broadcast_to([P, KT, P])
            nc.vector.tensor_copy(bvH, bv_all).then_inc(bv_high, 1)
            dve.wait_ge(bv_high, 1)
            nc.vector.tensor_tensor(bvL, bv_all, bvH.bitcast(f32), ALU.subtract).then_inc(bv_low, 1)
            nc.vector.memset(val[:, :, :, 3 * HEAD:VPITCH], 1.0).then_inc(ones_ok, 1)
            for c, (_, slot, factor, half) in enumerate(CHUNKS):
                if c == FIRST_REUSE:
                    for m in range(KT):
                        dve.wait_ge(merged_hi, m + 1)
                        nc.vector.tensor_tensor(WL["wm"][:, m, :], ring[m % RING][:],
                                                WH["wm"][:, m, :].bitcast(f32), ALU.subtract
                                                ).then_inc(merged_lo, 1)
                dve.wait_ge(w_high, c + 1)
                tiles = slice(2 * half, 2 * half + 2)
                nc.vector.scalar_tensor_tensor(out=WL[slot][:, tiles, :], in0=buffers[c % 3][:],
                                               scalar=factor or 1.0,
                                               in1=WH[slot][:, tiles, :].bitcast(f32),
                                               op0=ALU.mult, op1=ALU.subtract).then_inc(w_low, 1)
            dve.wait_ge(bias_row, 1)
            nc.vector.tensor_tensor(out_bias[:], ring[1][:], out_bias[:], ALU.add
                                    ).then_inc(bias_ok, 1)

            def mask(u, b):
                if u == 0:
                    dve.wait_ge(far_ok, count(b, 1, 0))
                dve.wait_ge(mm["score"], count(b, HEADS, u))
                if u >= 2:
                    dve.wait_ge(mm["turn"], count(b, HEADS, u - 2))
                elif started(b - 1):
                    dve.wait_ge(mm["turn"], count(b - 1, HEADS, HEADS + u - 2))
                settle(dve, dve_settled)
                for q in range(QT):
                    last = nc.vector.tensor_tensor_reduce(
                        out=probs[:, u % 2, q, :], in0=score[u % 2][:, q * NODES:(q + 1) * NODES],
                        in1=far[:, q, :], scale=1.0, scalar=FAR, op0=ALU.add, op1=ALU.min,
                        accum_out=least[:, u % 2, q:q + 1])
                last.then_inc(masked, 1)

            def turned_low(u, b):
                dve.wait_ge(hi["p"], count(b, HEADS, u))
                nc.vector.tensor_tensor(pL[:, u % 2, :, :],
                                        turned[u % 2][:].rearrange("p (k n) -> p k n", k=QT),
                                        pH[:, u % 2, :, :], ALU.subtract).then_inc(lo["p"], 1)

            def sum_parts(pair, b):
                dve.wait_ge(mm["pv"], count(b, HEADS, 2 * pair + 1))
                if pair >= 2:
                    dve.wait_ge(head_ok, count(b, HEADS // 2, pair - 2))
                elif started(b - 1):
                    dve.wait_ge(head_ok, count(b - 1, HEADS // 2, HEADS // 2 + pair - 2))
                nc.vector.reciprocal(o_rcp[:, pair % 2, :], pv4[:, :, 3 * HEAD])
                parts = pv4[:, :, 0:3 * HEAD].rearrange("p g (b d) -> p g d b", d=HEAD)
                nc.vector.tensor_reduce(o_sum[:, pair % 2, :, :], parts, AX.X, ALU.add
                                        ).then_inc(summed, 1)

            def tile_stats(which, src, q):
                nc.vector.bn_stats(stats[which][:, q, :], src[:, q, :]).then_inc(stat[which], 1)

            def aggregate(which, b):
                for q in range(QT):
                    dve.wait_ge(stat[which], count(b, QT, q))
                    settle(dve, dve_settled)
                    last = nc.vector.bn_aggr(meanvar[which][:, q, :], stats[which][:, q, :])
                last.then_inc(var_ok[which], 1)

            def first_stats(b):
                dve.wait_ge(xa_in, count(b, 16, 15))
                for q in range(QT):
                    tile_stats(0, xa, q)
                aggregate(0, b)
                reciprocal_deviation(0, b)

            def reciprocal_deviation(which, b):
                v, y = newton[which][:, 0, :], rstd[which][:]
                a, c = newton[which][:, 1, :], newton[which][:, 2, :]
                at = [0]

                def step(ins):
                    ins.then_inc(nstep[which], 1)
                    at[0] += 1
                    if at[0] < NSTEPS:
                        dve.wait_ge(nstep[which], count(b, NSTEPS, at[0] - 1))

                dve.wait_ge(var_ok[which], count(b, 1, 0))
                step(nc.vector.tensor_scalar(v, meanvar[which][:, :, 1], EPS, None, ALU.add))
                step(nc.vector.tensor_scalar(y.bitcast(i32), v.bitcast(i32), -0.5,
                                             float(RSQRT_SEED), ALU.mult, ALU.add))
                for _ in range(NEWTON_ROUNDS):
                    step(nc.vector.tensor_tensor(a, y, y, ALU.mult))
                    step(nc.vector.scalar_tensor_tensor(out=c, in0=a, scalar=-0.5, in1=v,
                                                        op0=ALU.mult, op1=ALU.mult))
                    step(nc.vector.scalar_tensor_tensor(out=y, in0=c, scalar=1.5, in1=y,
                                                        op0=ALU.add, op1=ALU.mult))

            def normalise(which, src, dst, b):
                dve.wait_ge(nstep[which], count(b, NSTEPS, NSTEPS - 1))
                for q in range(QT):
                    nc.vector.tensor_scalar(dst[:, q, :], src[:, q, :], meanvar[which][:, q, 0:1],
                                            rstd[which][:, q:q + 1], ALU.subtract, ALU.mult
                                            ).then_inc(normed[which], 1)

            def relu_low(dst, src, high, done):
                nc.vector.scalar_tensor_tensor(out=dst, in0=src, scalar=0.0,
                                               in1=high.bitcast(f32), op0=ALU.max,
                                               op1=ALU.subtract).then_inc(done, 1)

            def dense_low(name, b):
                k = int(name[-1]) if name != "al" else 0
                src = ring[BANK[name]]
                tok = slice(k * P, (k + 1) * P)
                if name.startswith("h1"):
                    dve.wait_ge(hi["h1"], count(b, 2, k))
                    relu_low(h1L[:, :, tok], src[:].rearrange("p (d n) -> p d n", d=KT),
                             h1H[:, :, tok], lo["h1"])
                elif name.startswith("h2"):
                    dve.wait_ge(hi["h2"], count(b, 2, k))
                    relu_low(h2L[:, :, tok], src[:].rearrange("p (d n) -> p d n", d=KT),
                             h2H[:, :, tok], lo["h2"])
                elif name.startswith("qk"):
                    dve.wait_ge(hi["qk"], count(b, 4, k))
                    nc.vector.scalar_tensor_tensor(
                        out=stage[:, k % 2, 1, :], in0=src[:, 0:NODES], scalar=bias_q[:, k:k + 1],
                        in1=stage[:, k % 2, 0, :].bitcast(f32), op0=ALU.add, op1=ALU.subtract)
                    nc.vector.scalar_tensor_tensor(
                        out=stage[:, k % 2, 3, :], in0=src[:, NODES:2 * NODES],
                        scalar=bias_k[:, k:k + 1], in1=stage[:, k % 2, 2, :].bitcast(f32),
                        op0=ALU.add, op1=ALU.subtract).then_inc(lo["qk"], 1)
                elif name.startswith("v"):
                    dve.wait_ge(hi["v"], count(b, 2, k))
                    if k == 1:
                        dve.wait_ge(v_low, count(b, 2, 0))
                    elif started(b - 1):
                        dve.wait_ge(v_low, count(b - 1, 2, 1))
                    nc.vector.tensor_tensor(
                        v_rest[:].rearrange("p q (h d) -> p q h d", d=HEAD),
                        src[:].rearrange("p (q h d) -> p q h d", q=QT, d=HEAD),
                        val[:, :, 8 * k:8 * k + 8, 2 * HEAD:3 * HEAD], ALU.subtract
                        ).then_inc(lo["v"], 1)
                elif name.startswith("ot"):
                    dve.wait_ge(hi["ot"], count(b, 2, k))
                    nc.vector.tensor_tensor(oL[:, 2 * k:2 * k + 2, :],
                                            src[:].rearrange("p (c n) -> p c n", c=2),
                                            oH[:, 2 * k:2 * k + 2, :].bitcast(f32), ALU.subtract
                                            ).then_inc(lo["ot"], 1)
                elif name.startswith("wo"):
                    dve.wait_ge(mm["wo"], count(b, 2, k))
                    if k == 0:
                        dve.wait_ge(x1_ok, count(b, 1, 0))
                    nc.vector.tensor_tensor(x1[:, k, :], src[:], x1[:, k, :], ALU.add
                                            ).then_inc(added, 1)
                    dve.wait_ge(added, count(b, 2, k))
                    tile_stats(1, x1, k)
                elif name.startswith("hw"):
                    dve.wait_ge(hi["hw"], count(b, 2, k))
                    nc.vector.tensor_tensor(hwL[:, k, :], src[:], hwH[:, k, :].bitcast(f32),
                                            ALU.subtract).then_inc(lo["hw"], 1)
                elif name.startswith("g"):
                    dve.wait_ge(hi["g"], count(b, 2, k))
                    nc.vector.tensor_tensor(gL[:, 2 * k:2 * k + 2, :],
                                            src[:].rearrange("p (c n) -> p c n", c=2),
                                            gH[:, 2 * k:2 * k + 2, :].bitcast(f32), ALU.subtract
                                            ).then_inc(lo["g"], 1)
                elif name == "al":
                    dve.wait_ge(mm["al"], count(b, 1, 0))
                    dve.wait_ge(keep_ok, count(b, 1, 0))
                    nc.vector.scalar_tensor_tensor(
                        out=work[:, 0, :].rearrange("p (m n) -> p m n", m=QT),
                        in0=src[:].rearrange("p (m n) -> p m n", m=QT), scalar=0.0, in1=keep[:],
                        op0=ALU.max, op1=ALU.mult).then_inc(l1_masked, 1)
                    dve.wait_ge(l1_masked, count(b, 1, 0))
                    nc.vector.tensor_reduce(l1_max[:], work[:, 0, :].rearrange(
                        "p (m n) -> p m n", m=QT), AX.X, ALU.max, negate=True).then_inc(l1_maxed, 1)
                elif name.startswith("av"):
                    dve.wait_ge(mm["av"], count(b, 2, k))
                    nc.vector.tensor_tensor(x1[:, k, :], src[:], x1[:, k, :], ALU.add
                                            ).then_inc(final, 1)

            def second_softmax(s, b):
                if s == AL_STEP + 1:
                    dve.wait_ge(l1_exped, count(b, 1, 0))
                    nc.vector.reciprocal(l1_rcp[:], l1_sum[:]).then_inc(l1_rcped, 1)
                if s == AL_STEP + 2:
                    dve.wait_ge(hi["e"], count(b, 1, 0))
                    for m in range(QT):
                        last = nc.vector.scalar_tensor_tensor(
                            out=eL[:, m, :], in0=work[:, 1, m * NODES:(m + 1) * NODES],
                            scalar=l1_rcp[:, m:m + 1], in1=eH[:, m, :].bitcast(f32),
                            op0=ALU.mult, op1=ALU.subtract)
                    last.then_inc(lo["e"], 1)

            def body(t, prev, cur, nxt, later):
                p, n = t - 1, t + 1
                present = {-1: prev, 0: cur, 1: nxt}
                for s in range(HEADS):
                    if cur and s + AHEAD < HEADS:
                        mask(s + AHEAD, t)
                    elif nxt and s + AHEAD >= HEADS:
                        if s + AHEAD == HEADS:
                            dve.wait_ge(far_next_ok, count(n, 1, 0))
                            if cur:
                                dve.wait_ge(masked, count(t, HEADS, HEADS - 1))
                            nc.vector.tensor_copy(far[:], far_next[:]).then_inc(far_ok, 1)
                        mask(s + AHEAD - HEADS, n)
                    if cur:
                        turned_low(s, t)
                    if s == 0 and prev:
                        sum_parts(HEADS // 2 - 1, p)
                    elif s > 0 and s % 2 == 0 and cur:
                        sum_parts(s // 2 - 1, t)
                    if s == STATS1 and later:
                        first_stats(n + 1)
                    if s == VAR2 and prev:
                        aggregate(1, p)
                        reciprocal_deviation(1, p)
                    if s == NORM2 and prev:
                        normalise(1, x1, work, p)
                    if s == NORM1 and later:
                        normalise(0, xa, xa, n + 1)
                    if prev:
                        second_softmax(s, p)
                    for name in DENSE[s]:
                        if present[ROLE[name]]:
                            dense_low(name, t + ROLE[name])

            first_stats(0)
            normalise(0, xa, xa, 0)
            sweep(dve, body)

        @block.gpsimd
        def _(pool):
            nc.gpsimd.memset(ident[:], 0.0).then_inc(ident_ok, 1)
            pool.wait_ge(ident_ok, 1)
            nc.gpsimd.affine_select(out=ident[:], in_=ident[:], compare_op=ALU.not_equal, fill=1.0,
                                    base=0, pattern=[[-1, P]], channel_multiplier=1
                                    ).then_inc(ident_ok, 1)

            def values_low(half, b):
                pool.wait_ge(v_mid, count(b, 2, half))
                heads = slice(8 * half, 8 * half + 8)
                rest = v_rest[:].rearrange("p q (h d) -> p q h d", d=HEAD)
                for q in range(QT):
                    last = nc.gpsimd.tensor_tensor(val[:, q, heads, 0:HEAD], rest[:, q, :, :],
                                                   val[:, q, heads, HEAD:2 * HEAD], ALU.subtract)
                last.then_inc(v_low, 1)

            def norm_heads(pair, b):
                pool.wait_ge(summed, count(b, HEADS // 2, pair))
                if started(b - 1):
                    pool.wait_ge(mm["ot"], count(b - 1, 2, pair // 4))
                for q in range(QT):
                    at = 2 * pair * HEAD
                    dst = heads_out[:, q, at:at + 2 * HEAD].rearrange("p (h d) -> p h d", h=2)
                    last = nc.gpsimd.tensor_tensor(
                        dst, o_sum[:, pair % 2, q:q + 3:2, :],
                        o_rcp[:, pair % 2, q:q + 3:2].unsqueeze(2).broadcast_to([P, 2, HEAD]),
                        ALU.mult)
                last.then_inc(head_ok, 1)

            def body(t, prev, cur, nxt, later):
                p, n = t - 1, t + 1
                for s in range(HEADS):
                    if s == MID[0] and nxt:
                        values_low(0, n)
                    if s == 0 and prev:
                        norm_heads(HEADS // 2 - 1, p)
                    elif s > 0 and s % 2 == 0 and cur:
                        norm_heads(s // 2 - 1, t)
                    if s == MID[1] and cur:
                        values_low(1, t)
                    if s == X1_STEP and prev:
                        pool.wait_ge(x1_in, count(p, 16, 15))
                        for q in range(QT):
                            last = nc.gpsimd.tensor_tensor(x1[:, q, :], x1[:, q, :], out_bias[:],
                                                           ALU.add)
                        last.then_inc(x1_ok, 1)
                    if s == KEEP_STEP and prev:
                        pool.wait_ge(adjt_got, count(p, 16, 15))
                        if started(p - 1):
                            pool.wait_ge(l1_masked, count(p - 1, 1, 0))
                        settle(pool, pool_settled)
                        for q in range(QT):
                            last = nc.gpsimd.tensor_scalar(keep[:, q, :], adjt_in[:, q, :], 0, 0,
                                                           ALU.is_equal, ALU.is_equal)
                        last.then_inc(keep_ok, 1)
                    if s == FAR_STEP and nxt:
                        pool.wait_ge(adj_got, count(n, 16, 15))
                        if started(t):
                            pool.wait_ge(far_ok, count(t, 1, 0))
                        settle(pool, pool_settled)
                        for q in range(QT):
                            last = nc.gpsimd.tensor_scalar(far_next[:, q, :], adj_in[:, q, :], 0,
                                                           FAR, ALU.is_equal, ALU.mult)
                        last.then_inc(far_next_ok, 1)

            sweep(pool, body)


def kernel(**inputs):
    import numpy as np
    import concourse.bacc as bacc
    from concourse.bass_utils import run_bass_kernel_spmd

    def columns(v):
        return np.ascontiguousarray(np.asarray(v).reshape(KT, P).T)

    src = {k: np.asarray(v) for k, v in inputs.items()}
    arrays = {
        "x": src["x"],
        "adj": src["adj"],
        "adj_t": np.ascontiguousarray(src["adj"].transpose(0, 2, 1)),
        "wq": src["L0_gnn_Wq"], "wk": src["L0_gnn_Wk"], "wv": src["L0_gnn_Wv"],
        "wo": src["L0_gnn_Wo"],
        "bq": columns(src["L0_gnn_bq"]), "bk": columns(src["L0_gnn_bk"]),
        "bv": columns(src["L0_gnn_bv"]), "bo": src["L0_gnn_bo"].reshape(1, DIM),
        "w1": src["L1_gnn_weight"],
        "wq1_t": np.ascontiguousarray(src["L1_gnn_wq"].T),
        "wk1_t": np.ascontiguousarray(src["L1_gnn_wk"].T),
    }
    nc = bacc.Bacc("TRN2", target_bir_lowering=False, num_devices=1)
    args = {n: nc.dram_tensor(f"{n}_dram", a.shape, mybir.dt.from_np(a.dtype),
                              kind="ExternalInput").ap() for n, a in arrays.items()}
    out = nc.dram_tensor("out_dram", (BATCH, NODES, DIM), mybir.dt.float32,
                         kind="ExternalOutput").ap()
    two_layers(nc, **args, out=out)
    r = run_bass_kernel_spmd(nc, [{f"{n}_dram": a for n, a in arrays.items()}], core_ids=[0])
    return r.results[0]["out_dram"]
```

```python
import concourse.bass as bass
from concourse import mybir
from contextlib import ExitStack

BATCH, NODES, DIM, HEADS = 32, 256, 512, 16
HEAD = DIM // HEADS
P = 128
KT = DIM // P
QT = NODES // P
GROUP = P // HEAD
VCOLS = 3 * HEAD + 1
VPITCH = VCOLS + 1
SCALE = HEAD ** -0.5
EPS = 1e-5
FAR = 3.0e38
RSQRT_SEED = 0x5F3759DF
NEWTON_ROUNDS = 3
NSTEPS = (3 + 4 * NEWTON_ROUNDS, 2 + 3 * NEWTON_ROUNDS)

DENSE = [
    ["qk2a"],
    ["ot1", "qk2b"],
    ["wo0a", "wo0b"],
    ["wo1"],
    ["qk3"],
    ["v1", "h2_0", "h2_1"],
    ["h1_0", "h1_1", "g0"],
    ["g1"],
    ["hw0"],
    ["qk0"],
    ["al"],
    ["v0a"],
    ["hw1"],
    ["v0b", "av0"],
    ["av1", "qk1a"],
    ["ot0", "qk1b"],
]
RING = 3
AHEAD = 2


def tile(name):
    return name.rstrip("ab")


def step_of(name):
    return next(s for s, names in enumerate(DENSE) if name in names or name + "b" in names)


ORDER = [name for step in DENSE for name in step if not name.endswith("b")]
assert len(ORDER) % RING == 0 and len(DENSE) == HEADS
BANK = {tile(name): i % RING for i, name in enumerate(ORDER)}
ROLE = {"v1": 0, "ot1": -1, "qk2": 0, "wo0": -1, "wo1": -1, "qk3": 0, "h2_0": -1, "h2_1": -1,
        "hw0": -1, "g0": -1, "g1": -1, "h1_0": 1, "h1_1": 1, "hw1": -1, "qk0": 1, "al": -1,
        "av0": -1, "av1": -1, "qk1": 1, "ot0": 0, "v0": 1}
for name in ORDER:
    if name.endswith("a"):
        first = next(s for s, names in enumerate(DENSE) if name in names)
        ROLE[name] = ROLE[tile(name)] + (first > step_of(tile(name)))
        ROLE[tile(name) + "b"] = ROLE[tile(name)]
AL_STEP = step_of("al")
MID = (step_of("v0") + 1, step_of("v1") + 1)
STATS1, VAR1, NORM1 = (7, 9), 9, 12
VAR2, NORM2 = 4, 5
X1_STEP, KEEP_STEP, FAR_STEP = 1, 3, 10
SPARE = [tile(name) for name in ORDER if tile(name) in ("hw0", "hw1", "g0", "g1", "al")]
FIRST, EARLY = 4, 6
CHUNK_STEPS = [0, 2, 3, 5, 7, 8, 10, 11]
assert CHUNK_STEPS[3] < step_of(SPARE[0]) and CHUNK_STEPS[5] < step_of(SPARE[KT])
assert CHUNK_STEPS[6] >= step_of(SPARE[KT - 1])


def count(graph, per_graph, k):
    return graph * per_graph + (k + 1)


def started(graph):
    return not (isinstance(graph, int) and graph < 0)


def bank_before(name, t):
    at, shift = ORDER.index(name), 0
    while True:
        at -= RING
        if at < 0:
            at, shift = at + len(ORDER), shift - 1
        other = ORDER[at]
        graph = t + shift + ROLE[other]
        if t + shift == 0 and tile(other) in SPARE:
            return other, -1 - t
        if t + shift < -1:
            return None, 0
        if 0 <= graph < BATCH:
            return other, graph - t


def two_layers(nc, x, adj, adj_t, wq, wk, wv, wo, bq, bk, bv, bo, w1, wq1_t, wk1_t, out):
    f32, f32r = mybir.dt.float32, mybir.dt.float32r
    bf16, f16, i32 = mybir.dt.bfloat16, mybir.dt.float16, mybir.dt.int32
    ALU, ACT, AX = mybir.AluOpType, mybir.ActivationFunctionType, mybir.AxisListType

    x_v = x.rearrange("b (q p) d -> b p q d", p=P)
    out_v = out.rearrange("b (q p) d -> b p q d", p=P)
    adj_v = adj.rearrange("b (q p) k -> b p q k", p=P)
    adjt_v = adj_t.rearrange("b (q p) k -> b p q k", p=P)

    ctx = ExitStack()
    with ctx:
        def sb(name, shape, dt):
            return ctx.enter_context(nc.sbuf_tensor(name, shape, dt))

        def bank(name):
            return ctx.enter_context(nc.psum_tensor(name, [P, 512], f32))

        def sem(name):
            return ctx.enter_context(nc.semaphore(name))

        WH = {n: sb(f"{n}_hi", [P, KT, DIM], f32r) for n in ("wq", "wk", "wv", "wo", "wm", "w1")}
        WL = {n: sb(f"{n}_lo", [P, KT, DIM], f32r) for n in ("wq", "wk", "wv", "wo", "wm", "w1")}
        ident = sb("ident", [P, P], f32)
        bias_q = sb("bias_q", [P, KT], f32)
        bias_k = sb("bias_k", [P, KT], f32)
        bias_v = sb("bias_v", [P, KT], f32)
        out_bias = sb("out_bias", [P, DIM], f32)

        xa = sb("xa", [P, QT, DIM], f32)
        x1 = sb("x1", [P, QT, DIM], f32)
        adj_in = sb("adj_in", [P, QT, NODES], i32)
        adjt_in = sb("adjt_in", [P, QT, NODES], i32)
        far_next = sb("far_next", [P, QT, NODES], bf16)
        far = sb("far", [P, QT, NODES], bf16)
        keep = sb("keep", [P, QT, NODES], bf16)
        h1H = sb("h1_hi", [P, KT, NODES], f32r)
        h1L = sb("h1_lo", [P, KT, NODES], f32r)
        stage = sb("stage", [P, 2, 4, NODES], f32r)
        stack = sb("stack", [P, 2, GROUP, 2, NODES], f32r)
        val = sb("val", [P, QT, HEADS, VPITCH], bf16)
        v_rest = sb("v_rest", [P, QT, NODES], f32)
        probs = sb("probs", [P, 2, QT, NODES], f32)
        least = sb("least", [P, 2, QT], f32)
        pH = sb("probs_t_hi", [P, 2, QT, NODES], f16)
        pL = sb("probs_t_lo", [P, 2, QT, NODES], f16)
        o_sum = sb("o_sum", [P, 2, 4, HEAD], f32)
        o_rcp = sb("o_rcp", [P, 2, 4], f32)
        heads_out = sb("heads_out", [P, QT, DIM], f32)
        oH = sb("heads_t_hi", [P, KT, NODES], f32r)
        oL = sb("heads_t_lo", [P, KT, NODES], f32r)
        work = sb("work", [P, QT, DIM], f32)
        h2H = sb("h2_hi", [P, KT, NODES], f32r)
        h2L = sb("h2_lo", [P, KT, NODES], f32r)
        gH = sb("g_hi", [P, KT, NODES], f32r)
        gL = sb("g_lo", [P, KT, NODES], f32r)
        hwH = sb("hw_hi", [P, QT, DIM], f32r)
        hwL = sb("hw_lo", [P, QT, DIM], f32r)
        eH = sb("e_hi", [P, QT, NODES], f32r)
        eL = sb("e_lo", [P, QT, NODES], f32r)
        l1_max = sb("l1_max", [P, QT], f32)
        l1_sum = sb("l1_sum", [P, QT], f32)
        l1_rcp = sb("l1_rcp", [P, QT], f32)
        stats = [sb(f"stats{n}", [P, QT, 6], f32) for n in (1, 2)]
        meanvar = [sb(f"meanvar{n}", [P, QT, 2], f32) for n in (1, 2)]
        rstd = [sb(f"rstd{n}", [P, QT], f32) for n in (1, 2)]
        newton = [sb(f"newton{n}", [P, 3, QT], f32) for n in (1, 2)]

        score = [bank("score0"), bank("score1")]
        turned = [bank("turned0"), bank("turned1")]
        pv = bank("pv")
        ring = [bank(f"ring{i}") for i in range(RING)]
        pv4 = pv[:, 0:4 * VPITCH].rearrange("p (g c) -> p g c", c=VPITCH)

        xa_in, x1_in = sem("xa_in"), sem("x1_in")
        adj_got, adjt_got = sem("adj_got"), sem("adjt_got")
        stacked = [[sem(f"stacked{par}{i}") for i in range(GROUP)] for par in range(2)]
        stored = sem("stored")
        small_in = sem("small_in")
        chunk_in = [sem(f"chunk_in{i}") for i in range(4)]
        ident_ok, ones_ok = sem("ident_ok"), sem("ones_ok")
        w_high, w_low = sem("w_high"), sem("w_low")
        bv_high, bv_low = sem("bv_high"), sem("bv_low")
        merged = sem("merged")
        merged_hi, merged_lo = sem("merged_hi"), sem("merged_lo")
        bias_q_ok = sem("bias_q_ok")
        mm = {n: sem(f"mm_{n}") for n in
              ("h1", "qk", "v", "score", "turn", "pv", "ot", "wo", "h2", "g", "al", "hw", "av")}
        hi = {n: sem(f"hi_{n}") for n in ("h1", "qk", "v", "p", "ot", "h2", "g", "e", "hw")}
        v_mid, exped, l1_exped = sem("v_mid"), sem("exped"), sem("l1_exped")
        lo = {n: sem(f"lo_{n}") for n in ("h1", "qk", "v", "p", "ot", "h2", "g", "e", "hw")}
        masked, summed = sem("masked"), sem("summed")
        added, l1_masked, l1_maxed, l1_rcped, final = (
            sem("added"), sem("l1_masked"), sem("l1_maxed"), sem("l1_rcped"), sem("final"))
        stat = [sem("stat1"), sem("stat2")]
        var_ok = [sem("var_ok1"), sem("var_ok2")]
        normed = [sem("normed1"), sem("normed2")]
        far_ok = sem("far_ok")
        v_low, head_ok = sem("v_low"), sem("head_ok")
        nstep = [sem("nstep1"), sem("nstep2")]
        dve_settled, pool_settled = sem("dve_settled"), sem("pool_settled")
        x1_ok, keep_ok, far_next_ok = sem("x1_ok"), sem("keep_ok"), sem("far_next_ok")

        RELEASE = {"v1": (lo["v"], 2, 1), "v0": (lo["v"], 2, 0),
                   "ot0": (lo["ot"], 2, 0), "ot1": (lo["ot"], 2, 1),
                   "wo0": (added, 2, 0), "wo1": (added, 2, 1),
                   "h1_0": (lo["h1"], 2, 0), "h1_1": (lo["h1"], 2, 1),
                   "h2_0": (lo["h2"], 2, 0), "h2_1": (lo["h2"], 2, 1),
                   "g0": (lo["g"], 2, 0), "g1": (lo["g"], 2, 1), "al": (l1_masked, 1, 0),
                   "hw0": (lo["hw"], 2, 0), "hw1": (lo["hw"], 2, 1),
                   "av0": (final, 2, 0), "av1": (final, 2, 1),
                   "qk0": (lo["qk"], 4, 0), "qk1": (lo["qk"], 4, 1),
                   "qk2": (lo["qk"], 4, 2), "qk3": (lo["qk"], 4, 3)}

        CHUNKS = [(src, slot, factor, half)
                  for src, slot, factor in ((wq, "wq", -SCALE), (wk, "wk", None), (wv, "wv", None),
                                            (wk1_t, "wk1_t", None), (wq1_t, "w1", None),
                                            (wo, "wo", None), (w1, "w1", None))
                  for half in range(2)]
        buffers = [x1[:], work[:], heads_out[:],
                   probs[:].rearrange("p u q n -> p u (q n)")]

        def buffer_of(c):
            return c if c < FIRST else c % 2

        def arrival(c):
            at = buffer_of(c)
            return chunk_in[at], 16 * sum(buffer_of(other) == at for other in range(c + 1))

        def split_parts(c):
            _, slot, _, half = CHUNKS[c]
            tiles, src = slice(2 * half, 2 * half + 2), buffers[buffer_of(c)]
            if slot == "wk1_t":
                return [(gH[:, tiles, :], h2H[:, tiles, :], src[:, :, 0:NODES]),
                        (gL[:, tiles, :], h2L[:, tiles, :], src[:, :, NODES:2 * NODES])]
            return [(WH[slot][:, tiles, :], WL[slot][:, tiles, :], src)]

        def load_chunk(engine, c):
            src, _, _, half = CHUNKS[c]
            engine.dma_start(buffers[buffer_of(c)],
                             src.rearrange("(k p) n -> p k n", p=P)[:, 2 * half:2 * half + 2, :]
                             ).then_inc(arrival(c)[0], 16)

        block = ctx.enter_context(nc.Block())

        def settle(engine, settled):
            engine.sem_inc(settled, 1)

        def sweep(engine, body):
            body(-1, False, False, True, True)
            body(0, False, True, True, True)
            body(1, True, True, True, True)
            with engine.Fori(2, BATCH - 2) as t:
                body(t, True, True, True, True)
            body(BATCH - 2, True, True, True, False)
            body(BATCH - 1, True, True, False, False)
            body(BATCH, True, False, False, False)

        @block.sync
        def _(sp):
            sp.dma_start(xa[:], x_v[0, :, :, :]).then_inc(xa_in, 16)
            sp.dma_start(bias_q[:], bq).then_inc(small_in, 16)
            sp.dma_start(bias_k[:], bk).then_inc(small_in, 16)
            sp.dma_start(bias_v[:], bv).then_inc(small_in, 16)
            sp.dma_start(out_bias[:], bo.broadcast_to([P, DIM])).then_inc(small_in, 16)
            for c in range(EARLY + 2):
                if c >= FIRST:
                    sp.wait_ge(w_low, 1 + max(o for o in range(c) if buffer_of(o) == buffer_of(c)))
                load_chunk(sp, c)

            def stack_heads(g, b):
                par = g % 2
                sp.wait_ge(lo["qk"], count(b, 4, g))
                for i in range(GROUP):
                    for j in range(4):
                        first, second = j // 2, 2 + j % 2
                        sp.dma_start(
                            stack[HEAD * j:HEAD * (j + 1), par, i, :, :].bitcast(f32),
                            stage[HEAD * i:HEAD * (i + 1), par, first:second + 1:second - first, :]
                            .bitcast(f32)).then_inc(stacked[par][i], 16)

            def body(t, prev, cur, nxt, later):
                p, n = t - 1, t + 1
                if nxt:
                    if started(t):
                        sp.wait_ge(far_next_ok, count(t, 1, 0))
                    sp.dma_start(adj_in[:], adj_v[n, :, :, :]).then_inc(adj_got, 16)
                if prev:
                    if started(p - 1):
                        sp.wait_ge(keep_ok, count(p - 1, 1, 0))
                    sp.dma_start(adjt_in[:], adjt_v[p, :, :, :]).then_inc(adjt_got, 16)
                if cur:
                    stack_heads(1, t)
                    stack_heads(2, t)
                    stack_heads(3, t)
                if nxt:
                    stack_heads(0, n)
                if prev:
                    sp.wait_ge(final, count(p, 2, 1))
                    sp.dma_start(out_v[p, :, :, :], x1[:]).then_inc(stored, 16)

            sweep(sp, body)
            sp.wait_ge(stored, 16 * BATCH)

        @block.tensor
        def _(pe):
            def product(dst, parts, tiles, halves=(0, 1)):
                last = None
                for k in range(halves[0] * tiles // 2, (halves[-1] + 1) * tiles // 2):
                    (aH, bH), (aL, bL) = parts(k)
                    steps = ((aH, bH), (aH, bL), (aL, bH))
                    for s, (a, b) in enumerate(steps):
                        last = nc.tensor.matmul(dst, a, b, start=(k == 0 and s == 0),
                                                stop=(k == tiles - 1 and s == 2))
                return last

            pe.wait_ge(ident_ok, 2)
            pe.wait_ge(ones_ok, 1)

            def merge(at, other, off):
                dst = ring[BANK[SPARE[at]]]
                s, per, idx = RELEASE[tile(other)]
                pe.wait_ge(s, count(off, per, idx)) if off >= 0 else pe.wait_ge(
                    merged_lo, SPARE.index(tile(other)) + 1)
                if at < KT:
                    pe.wait_ge(w_low, EARLY + 4)
                    high, low = (gH, h2H) if at < KT // 2 else (gL, h2L)
                    cols = slice((at % 2) * P, (at % 2 + 1) * P)
                    product(dst[:], lambda k: ((high[:, k, cols], WH["w1"][:, k, :]),
                                               (low[:, k, cols], WL["w1"][:, k, :])), KT
                            ).then_inc(merged, 1)
                else:
                    pe.wait_ge(bv_low, 1)
                    pe.wait_ge(w_low, EARLY + 6)
                    bvH = eH[:, :, :].rearrange("p a (b m) -> p (a b) m", m=P)
                    bvL = eL[:, :, :].rearrange("p a (b m) -> p (a b) m", m=P)
                    product(dst[:], lambda k: ((bvH[:, k, :], WH["wo"][:, k, :]),
                                               (bvL[:, k, :], WL["wo"][:, k, :])), KT
                            ).then_inc(merged, 1)

            def scores(u, b):
                g, i = u // GROUP, u % GROUP
                pe.wait_ge(stacked[g % 2][i], count(b, 2, g // 2) * (16 * 4))
                if u >= 2:
                    pe.wait_ge(masked, count(b, HEADS, u - 2))
                elif started(b - 1):
                    pe.wait_ge(masked, count(b - 1, HEADS, HEADS + u - 2))
                for q in range(QT):
                    last = nc.tensor.matmul(score[u % 2][:, q * NODES:(q + 1) * NODES],
                                            stack[:, g % 2, i, 0, q * P:(q + 1) * P],
                                            stack[:, g % 2, i, 1, :], start=True, stop=True)
                last.then_inc(mm["score"], 1)

            def turn(u, b):
                pe.wait_ge(exped, count(b, HEADS, u))
                if u >= 2:
                    pe.wait_ge(lo["p"], count(b, HEADS, u - 2))
                elif started(b - 1):
                    pe.wait_ge(lo["p"], count(b - 1, HEADS, HEADS + u - 2))
                for q in range(QT):
                    for k in range(QT):
                        at = k * NODES + q * P
                        last = nc.tensor.transpose(turned[u % 2][:, at:at + P],
                                                   probs[:, u % 2, q, k * P:(k + 1) * P], ident[:])
                last.then_inc(mm["turn"], 1)

            def weigh(u, b):
                pe.wait_ge(lo["p"], count(b, HEADS, u))
                if u % (HEADS // 2) == 0:
                    pe.wait_ge(v_low, count(b, 2, u // (HEADS // 2)))
                if u % 2 == 0:
                    if u >= 2:
                        pe.wait_ge(summed, count(b, HEADS // 2, u // 2 - 1))
                    elif started(b - 1):
                        pe.wait_ge(summed, count(b - 1, HEADS // 2, HEADS // 2 - 1))
                for q in range(QT):
                    slot = (u % 2) * QT + q
                    for k in range(QT):
                        cols = slice(q * P, (q + 1) * P)
                        nc.tensor.matmul(pv4[:, slot, 0:VCOLS], pH[:, u % 2, k, cols],
                                         val[:, k, u, 0:VCOLS], start=(k == 0), stop=False)
                        last = nc.tensor.matmul(pv4[:, slot, HEAD:VCOLS], pL[:, u % 2, k, cols],
                                                val[:, k, u, HEAD:VCOLS], start=False,
                                                stop=(k == QT - 1))
                last.then_inc(mm["pv"], 1)

            WEIGHTS_BY = {("qk0", 0): (w_low, 4), ("v0", 0): (w_low, EARLY),
                          ("wo0", 0): (w_low, EARLY + 6), ("wo1", 0): (w_low, EARLY + 6),
                          ("hw0", 0): (w_low, len(CHUNKS)), ("hw1", 0): (w_low, len(CHUNKS)),
                          ("g0", 0): (merged_lo, KT), ("g1", 0): (merged_lo, KT)}

            def dense(name, t, step_t):
                b = t + ROLE[name]
                halves = [h for h in range(2) if name[-1] != "ba"[h]]
                complete = not name.endswith("a")
                other, off = bank_before(name, step_t) if 0 in halves else (None, 0)
                name = tile(name)
                k = int(name[-1]) if name != "al" else 0
                dst = ring[BANK[name]]
                if other is not None and isinstance(t, int) and t + off < 0:
                    pe.wait_ge(merged_lo, SPARE.index(tile(other)) + 1)
                elif other is not None:
                    s, per, idx = RELEASE[tile(other)]
                    pe.wait_ge(s, count(t + off, per, idx))
                if isinstance(b, int) and (name, b) in WEIGHTS_BY:
                    pe.wait_ge(*WEIGHTS_BY[name, b])
                tok = slice(k * P, (k + 1) * P)

                def signal(last, kind):
                    if complete:
                        last.then_inc(mm[kind], 1)

                if name.startswith("h1"):
                    pe.wait_ge(normed[0], count(b, 2, k))
                    for d in range(KT):
                        last = nc.tensor.transpose(dst[:, d * P:(d + 1) * P],
                                                   xa[:, k, d * P:(d + 1) * P], ident[:])
                    last.then_inc(mm["h1"], 1)
                elif name.startswith("h2"):
                    pe.wait_ge(normed[1], count(b, 2, k))
                    for d in range(KT):
                        last = nc.tensor.transpose(dst[:, d * P:(d + 1) * P],
                                                   work[:, k, d * P:(d + 1) * P], ident[:])
                    last.then_inc(mm["h2"], 1)
                elif name.startswith("qk"):
                    pe.wait_ge(lo["h1"], count(b, 2, 1))
                    cols = slice(k * P, (k + 1) * P)
                    for half in halves:
                        w = ("wq", "wk")[half]
                        last = product(dst[:, half * NODES:(half + 1) * NODES],
                                       lambda d: ((WH[w][:, d, cols], h1H[:, d, :]),
                                                  (WL[w][:, d, cols], h1L[:, d, :])), KT)
                    signal(last, "qk")
                elif name.startswith("v"):
                    pe.wait_ge(lo["h1"], count(b, 2, 1))
                    cols = slice(k * NODES, (k + 1) * NODES)
                    for q in halves:
                        rows = slice(q * P, (q + 1) * P)
                        last = product(dst[:, q * NODES:(q + 1) * NODES],
                                       lambda d: ((h1H[:, d, rows], WH["wv"][:, d, cols]),
                                                  (h1L[:, d, rows], WL["wv"][:, d, cols])), KT)
                    signal(last, "v")
                elif name.startswith("ot"):
                    pe.wait_ge(head_ok, count(b, HEADS // 2, 4 * k + 3))
                    for c in range(2):
                        for q in range(QT):
                            at = c * NODES + q * P
                            last = nc.tensor.transpose(
                                dst[:, at:at + P],
                                heads_out[:, q, (2 * k + c) * P:(2 * k + c + 1) * P], ident[:])
                    last.then_inc(mm["ot"], 1)
                elif name.startswith("wo"):
                    pe.wait_ge(lo["ot"], count(b, 2, halves[-1]))
                    signal(product(dst[:], lambda d: ((oH[:, d, tok], WH["wo"][:, d, :]),
                                                      (oL[:, d, tok], WL["wo"][:, d, :])), KT,
                                   halves), "wo")
                elif name.startswith("hw"):
                    pe.wait_ge(lo["h2"], count(b, 2, k))
                    signal(product(dst[:], lambda d: ((h2H[:, d, tok], WH["w1"][:, d, :]),
                                                      (h2L[:, d, tok], WL["w1"][:, d, :])), KT,
                                   halves), "hw")
                elif name.startswith("g"):
                    pe.wait_ge(lo["h2"], count(b, 2, 1))
                    for c in halves:
                        cols = slice((2 * k + c) * P, (2 * k + c + 1) * P)
                        last = product(dst[:, c * NODES:(c + 1) * NODES],
                                       lambda d: ((WH["wm"][:, d, cols], h2H[:, d, :]),
                                                  (WL["wm"][:, d, cols], h2L[:, d, :])), KT)
                    signal(last, "g")
                elif name == "al":
                    pe.wait_ge(lo["g"], count(b, 2, 1))
                    for m in halves:
                        rows = slice(m * P, (m + 1) * P)
                        last = product(dst[:, m * NODES:(m + 1) * NODES],
                                       lambda d: ((gH[:, d, rows], h2H[:, d, :]),
                                                  (gL[:, d, rows], h2L[:, d, :])), KT)
                    signal(last, "al")
                else:
                    pe.wait_ge(lo["e"], count(b, 1, 0))
                    pe.wait_ge(lo["hw"], count(b, 2, 1))
                    product(dst[:], lambda m: ((eH[:, m, tok], hwH[:, m, :]),
                                               (eL[:, m, tok], hwL[:, m, :])), QT
                            ).then_inc(mm["av"], 1)

            def body(t, prev, cur, nxt, later):
                present = {-1: prev, 0: cur, 1: nxt}
                for s in range(HEADS):
                    if cur:
                        turn(s, t)
                    if cur and s + AHEAD < HEADS:
                        scores(s + AHEAD, t)
                    elif nxt and s + AHEAD >= HEADS:
                        scores(s + AHEAD - HEADS, t + 1)
                    if s == 0 and prev:
                        weigh(HEADS - 1, t - 1)
                    elif s > 0 and cur:
                        weigh(s - 1, t)
                    for name in DENSE[s]:
                        if present[ROLE[name]]:
                            dense(name, t, t if isinstance(t, int) else 2)
                        elif cur and tile(name) in SPARE and not name.endswith("b"):
                            merge(SPARE.index(tile(name)), *bank_before(name, t))

            for name in ORDER:
                assert len({bank_before(name, t) for t in range(2, BATCH - 2)}) == 1
            sweep(pe, body)

        @block.scalar
        def _(act):
            def chunk_high(c):
                act.wait_ge(*arrival(c))
                if c >= EARLY + 6:
                    act.wait_ge(merged, KT)
                for high, _, src in split_parts(c):
                    last = nc.scalar.activation(high, src, ACT.Copy, scale=CHUNKS[c][2] or 1.0)
                last.then_inc(w_high, 1)

            def merged_high(at):
                if at < KT:
                    act.wait_ge(merged, at + 1)
                    nc.scalar.activation(WH["wm"][:, at, :], ring[BANK[SPARE[at]]][:], ACT.Copy
                                         ).then_inc(merged_hi, 1)

            for c in range(FIRST):
                chunk_high(c)
            act.wait_ge(bias_q_ok, 1)
            act.wait_ge(small_in, 64)

            def exponentials(u, b):
                act.wait_ge(masked, count(b, HEADS, u))
                for q in range(QT):
                    last = nc.scalar.activation(probs[:, u % 2, q, :], probs[:, u % 2, q, :],
                                                ACT.Exp, bias=least[:, u % 2, q:q + 1], scale=-1.0)
                last.then_inc(exped, 1)

            def turned_high(u, b):
                act.wait_ge(mm["turn"], count(b, HEADS, u))
                if u >= 2:
                    act.wait_ge(mm["pv"], count(b, HEADS, u - 2))
                elif started(b - 1):
                    act.wait_ge(mm["pv"], count(b - 1, HEADS, HEADS + u - 2))
                nc.scalar.activation(pH[:, u % 2, :, :],
                                     turned[u % 2][:].rearrange("p (k n) -> p k n", k=QT),
                                     ACT.Copy).then_inc(hi["p"], 1)

            def values_mid(half, b):
                act.wait_ge(lo["v"], count(b, 2, half))
                rest = v_rest[:].rearrange("p q (h d) -> p q h d", d=HEAD)
                nc.scalar.activation(val[:, :, 8 * half:8 * half + 8, HEAD:2 * HEAD], rest,
                                     ACT.Copy).then_inc(v_mid, 1)

            def dense_high(name, b):
                k = int(name[-1]) if name != "al" else 0
                src = ring[BANK[name]]
                tok = slice(k * P, (k + 1) * P)
                if name.startswith("h1"):
                    act.wait_ge(mm["h1"], count(b, 2, k))
                    if started(b - 1):
                        act.wait_ge(mm["qk"], count(b - 1, 4, 3))
                        act.wait_ge(mm["v"], count(b - 1, 2, 1))
                    nc.scalar.activation(h1H[:, :, tok],
                                         src[:].rearrange("p (d n) -> p d n", d=KT),
                                         ACT.Relu).then_inc(hi["h1"], 1)
                elif name.startswith("h2"):
                    act.wait_ge(mm["h2"], count(b, 2, k))
                    if started(b - 1):
                        act.wait_ge(mm["al"], count(b - 1, 1, 0))
                    nc.scalar.activation(h2H[:, :, tok],
                                         src[:].rearrange("p (d n) -> p d n", d=KT),
                                         ACT.Relu).then_inc(hi["h2"], 1)
                elif name.startswith("qk"):
                    act.wait_ge(mm["qk"], count(b, 4, k))
                    if k >= 2 or started(b - 1):
                        act.wait_ge(mm["score"], count(b, HEADS, GROUP * (k - 1) - 1))
                    nc.scalar.activation(stage[:, k % 2, 0, :], src[:, 0:NODES], ACT.Identity,
                                         bias=bias_q[:, k:k + 1])
                    nc.scalar.activation(stage[:, k % 2, 2, :], src[:, NODES:2 * NODES],
                                         ACT.Identity, bias=bias_k[:, k:k + 1]
                                         ).then_inc(hi["qk"], 1)
                elif name.startswith("v"):
                    act.wait_ge(mm["v"], count(b, 2, k))
                    if started(b - 1):
                        act.wait_ge(mm["pv"], count(b - 1, HEADS, 8 * k + 7))
                    nc.scalar.activation(val[:, :, 8 * k:8 * k + 8, 2 * HEAD:3 * HEAD],
                                         src[:].rearrange("p (q h d) -> p q h d", q=QT, d=HEAD),
                                         ACT.Copy).then_inc(hi["v"], 1)
                elif name.startswith("ot"):
                    act.wait_ge(mm["ot"], count(b, 2, k))
                    if started(b - 1):
                        act.wait_ge(mm["wo"], count(b - 1, 2, 1))
                    nc.scalar.activation(oH[:, 2 * k:2 * k + 2, :],
                                         src[:].rearrange("p (c n) -> p c n", c=2),
                                         ACT.Copy).then_inc(hi["ot"], 1)
                elif name.startswith("hw"):
                    act.wait_ge(mm["hw"], count(b, 2, k))
                    if started(b - 1):
                        act.wait_ge(mm["av"], count(b - 1, 2, 1))
                    nc.scalar.activation(hwH[:, k, :], src[:], ACT.Copy).then_inc(hi["hw"], 1)
                elif name.startswith("g"):
                    act.wait_ge(mm["g"], count(b, 2, k))
                    if started(b - 1):
                        act.wait_ge(mm["al"], count(b - 1, 1, 0))
                    nc.scalar.activation(gH[:, 2 * k:2 * k + 2, :],
                                         src[:].rearrange("p (c n) -> p c n", c=2),
                                         ACT.Copy).then_inc(hi["g"], 1)

            def second_softmax(s, b):
                if s == AL_STEP + 1:
                    act.wait_ge(l1_maxed, count(b, 1, 0))
                    for m in range(QT):
                        last = nc.scalar.activation(work[:, 1, m * NODES:(m + 1) * NODES],
                                                    work[:, 0, m * NODES:(m + 1) * NODES], ACT.Exp,
                                                    bias=l1_max[:, m:m + 1],
                                                    accum_out=l1_sum[:, m:m + 1])
                    last.then_inc(l1_exped, 1)
                if s == AL_STEP + 2:
                    act.wait_ge(l1_rcped, count(b, 1, 0))
                    if started(b - 1):
                        act.wait_ge(mm["av"], count(b - 1, 2, 1))
                    for m in range(QT):
                        last = nc.scalar.activation(eH[:, m, :], work[:, 1, m * NODES:(m + 1) * NODES],
                                                    ACT.Copy, scale=l1_rcp[:, m:m + 1])
                    last.then_inc(hi["e"], 1)

            def body(t, prev, cur, nxt, later):
                p, n = t - 1, t + 1
                present = {-1: prev, 0: cur, 1: nxt}
                if prev:
                    if started(p - 1):
                        act.wait_ge(stored, count(p - 1, 16, 15))
                    else:
                        act.wait_ge(w_low, len(CHUNKS))
                    act.dma_start(x1[:], x_v[p, :, :, :]).then_inc(x1_in, 16)
                for s in range(HEADS):
                    if cur and s + 1 < HEADS:
                        exponentials(s + 1, t)
                    elif nxt and s + 1 == HEADS:
                        exponentials(0, t + 1)
                    if cur:
                        turned_high(s, t)
                    if s == MID[0] and nxt:
                        values_mid(0, n)
                    if s == MID[1] and cur:
                        values_mid(1, t)
                    if prev:
                        second_softmax(s, p)
                    for name in DENSE[s]:
                        if present[ROLE[name]] and not name.endswith("a"):
                            dense_high(tile(name), t + ROLE[name])
                        elif cur and not prev and tile(name) in SPARE and not name.endswith("a"):
                            merged_high(SPARE.index(tile(name)))
                    if nxt and not cur and s == step_of("h1_1"):
                        for c in range(FIRST, EARLY):
                            chunk_high(c)
                    if cur and not prev:
                        for c in range(EARLY, len(CHUNKS)):
                            if s == CHUNK_STEPS[c - EARLY]:
                                chunk_high(c)
                            if s == CHUNK_STEPS[c - EARLY] + 1 and c + 2 < len(CHUNKS):
                                act.wait_ge(w_low, c + 1)
                                load_chunk(act, c + 2)
                    if "h1_1" in DENSE[s] and later:
                        act.wait_ge(mm["h1"], count(n, 2, 1))
                        act.dma_start(xa[:], x_v[n + 1, :, :, :]).then_inc(xa_in, 16)

            sweep(act, body)

        @block.vector
        def _(dve):
            def chunk_low(c):
                dve.wait_ge(w_high, c + 1)
                for high, low, src in split_parts(c):
                    last = nc.vector.scalar_tensor_tensor(out=low, in0=src,
                                                          scalar=CHUNKS[c][2] or 1.0,
                                                          in1=high.bitcast(f32),
                                                          op0=ALU.mult, op1=ALU.subtract)
                last.then_inc(w_low, 1)

            def merged_low(at):
                src = ring[BANK[SPARE[at]]][:]
                if at < KT:
                    dve.wait_ge(merged_hi, at + 1)
                    nc.vector.tensor_tensor(WL["wm"][:, at, :], src,
                                            WH["wm"][:, at, :].bitcast(f32), ALU.subtract
                                            ).then_inc(merged_lo, 1)
                else:
                    dve.wait_ge(merged, at + 1)
                    nc.vector.tensor_tensor(out_bias[:], src, out_bias[:], ALU.add
                                            ).then_inc(merged_lo, 1)

            def mask(u, b):
                if u == 0:
                    dve.wait_ge(far_ok, count(b, 1, 0))
                dve.wait_ge(mm["score"], count(b, HEADS, u))
                if u >= 2:
                    dve.wait_ge(mm["turn"], count(b, HEADS, u - 2))
                elif started(b - 1):
                    dve.wait_ge(mm["turn"], count(b - 1, HEADS, HEADS + u - 2))
                settle(dve, dve_settled)
                for q in range(QT):
                    last = nc.vector.tensor_tensor_reduce(
                        out=probs[:, u % 2, q, :], in0=score[u % 2][:, q * NODES:(q + 1) * NODES],
                        in1=far[:, q, :], scale=1.0, scalar=FAR, op0=ALU.add, op1=ALU.min,
                        accum_out=least[:, u % 2, q:q + 1])
                last.then_inc(masked, 1)

            def turned_low(u, b):
                dve.wait_ge(hi["p"], count(b, HEADS, u))
                nc.vector.tensor_tensor(pL[:, u % 2, :, :],
                                        turned[u % 2][:].rearrange("p (k n) -> p k n", k=QT),
                                        pH[:, u % 2, :, :], ALU.subtract).then_inc(lo["p"], 1)

            def sum_parts(pair, b):
                dve.wait_ge(mm["pv"], count(b, HEADS, 2 * pair + 1))
                if pair >= 2:
                    dve.wait_ge(head_ok, count(b, HEADS // 2, pair - 2))
                elif started(b - 1):
                    dve.wait_ge(head_ok, count(b - 1, HEADS // 2, HEADS // 2 + pair - 2))
                nc.vector.reciprocal(o_rcp[:, pair % 2, :], pv4[:, :, 3 * HEAD])
                parts = pv4[:, :, 0:3 * HEAD].rearrange("p g (b d) -> p g d b", d=HEAD)
                nc.vector.tensor_reduce(o_sum[:, pair % 2, :, :], parts, AX.X, ALU.add
                                        ).then_inc(summed, 1)

            def tile_stats(which, src, q):
                nc.vector.bn_stats(stats[which][:, q, :], src[:, q, :]).then_inc(stat[which], 1)

            def aggregate(which, b):
                for q in range(QT):
                    dve.wait_ge(stat[which], count(b, QT, q))
                    settle(dve, dve_settled)
                    last = nc.vector.bn_aggr(meanvar[which][:, q, :], stats[which][:, q, :])
                last.then_inc(var_ok[which], 1)

            def first_stats(q, b):
                dve.wait_ge(xa_in, count(b, 16, 15))
                tile_stats(0, xa, q)
                if q == QT - 1:
                    aggregate(0, b)

            def reciprocal_deviation(b):
                v, y = newton[1][:, 0, :], rstd[1][:]
                a, c = newton[1][:, 1, :], newton[1][:, 2, :]
                at = [0]

                def step(ins):
                    ins.then_inc(nstep[1], 1)
                    at[0] += 1
                    if at[0] < NSTEPS[1]:
                        dve.wait_ge(nstep[1], count(b, NSTEPS[1], at[0] - 1))

                dve.wait_ge(var_ok[1], count(b, 1, 0))
                step(nc.vector.tensor_scalar(v, meanvar[1][:, :, 1], EPS, None, ALU.add))
                step(nc.vector.tensor_scalar(y.bitcast(i32), v.bitcast(i32), -0.5,
                                             float(RSQRT_SEED), ALU.mult, ALU.add))
                for _ in range(NEWTON_ROUNDS):
                    step(nc.vector.tensor_tensor(a, y, y, ALU.mult))
                    step(nc.vector.scalar_tensor_tensor(out=c, in0=a, scalar=-0.5, in1=v,
                                                        op0=ALU.mult, op1=ALU.mult))
                    step(nc.vector.scalar_tensor_tensor(out=y, in0=c, scalar=1.5, in1=y,
                                                        op0=ALU.add, op1=ALU.mult))

            def normalise(which, src, dst, b):
                dve.wait_ge(nstep[which], count(b, NSTEPS[which], NSTEPS[which] - 1))
                for q in range(QT):
                    nc.vector.tensor_scalar(dst[:, q, :], src[:, q, :], meanvar[which][:, q, 0:1],
                                            rstd[which][:, q:q + 1], ALU.subtract, ALU.mult
                                            ).then_inc(normed[which], 1)

            def relu_low(dst, src, high, done):
                nc.vector.scalar_tensor_tensor(out=dst, in0=src, scalar=0.0,
                                               in1=high.bitcast(f32), op0=ALU.max,
                                               op1=ALU.subtract).then_inc(done, 1)

            def dense_low(name, b):
                k = int(name[-1]) if name != "al" else 0
                src = ring[BANK[name]]
                tok = slice(k * P, (k + 1) * P)
                if name.startswith("h1"):
                    dve.wait_ge(hi["h1"], count(b, 2, k))
                    relu_low(h1L[:, :, tok], src[:].rearrange("p (d n) -> p d n", d=KT),
                             h1H[:, :, tok], lo["h1"])
                elif name.startswith("h2"):
                    dve.wait_ge(hi["h2"], count(b, 2, k))
                    relu_low(h2L[:, :, tok], src[:].rearrange("p (d n) -> p d n", d=KT),
                             h2H[:, :, tok], lo["h2"])
                elif name.startswith("qk"):
                    dve.wait_ge(hi["qk"], count(b, 4, k))
                    nc.vector.scalar_tensor_tensor(
                        out=stage[:, k % 2, 1, :], in0=src[:, 0:NODES], scalar=bias_q[:, k:k + 1],
                        in1=stage[:, k % 2, 0, :].bitcast(f32), op0=ALU.add, op1=ALU.subtract)
                    nc.vector.scalar_tensor_tensor(
                        out=stage[:, k % 2, 3, :], in0=src[:, NODES:2 * NODES],
                        scalar=bias_k[:, k:k + 1], in1=stage[:, k % 2, 2, :].bitcast(f32),
                        op0=ALU.add, op1=ALU.subtract).then_inc(lo["qk"], 1)
                elif name.startswith("v"):
                    dve.wait_ge(hi["v"], count(b, 2, k))
                    if k == 1:
                        dve.wait_ge(v_low, count(b, 2, 0))
                    elif started(b - 1):
                        dve.wait_ge(v_low, count(b - 1, 2, 1))
                    nc.vector.tensor_tensor(
                        v_rest[:].rearrange("p q (h d) -> p q h d", d=HEAD),
                        src[:].rearrange("p (q h d) -> p q h d", q=QT, d=HEAD),
                        val[:, :, 8 * k:8 * k + 8, 2 * HEAD:3 * HEAD], ALU.subtract
                        ).then_inc(lo["v"], 1)
                elif name.startswith("ot"):
                    dve.wait_ge(hi["ot"], count(b, 2, k))
                    nc.vector.tensor_tensor(oL[:, 2 * k:2 * k + 2, :],
                                            src[:].rearrange("p (c n) -> p c n", c=2),
                                            oH[:, 2 * k:2 * k + 2, :].bitcast(f32), ALU.subtract
                                            ).then_inc(lo["ot"], 1)
                elif name.startswith("wo"):
                    dve.wait_ge(mm["wo"], count(b, 2, k))
                    if k == 0:
                        dve.wait_ge(x1_ok, count(b, 1, 0))
                    nc.vector.tensor_tensor(x1[:, k, :], src[:], x1[:, k, :], ALU.add
                                            ).then_inc(added, 1)
                    dve.wait_ge(added, count(b, 2, k))
                    tile_stats(1, x1, k)
                elif name.startswith("hw"):
                    dve.wait_ge(hi["hw"], count(b, 2, k))
                    nc.vector.tensor_tensor(hwL[:, k, :], src[:], hwH[:, k, :].bitcast(f32),
                                            ALU.subtract).then_inc(lo["hw"], 1)
                elif name.startswith("g"):
                    dve.wait_ge(hi["g"], count(b, 2, k))
                    nc.vector.tensor_tensor(gL[:, 2 * k:2 * k + 2, :],
                                            src[:].rearrange("p (c n) -> p c n", c=2),
                                            gH[:, 2 * k:2 * k + 2, :].bitcast(f32), ALU.subtract
                                            ).then_inc(lo["g"], 1)
                elif name == "al":
                    dve.wait_ge(mm["al"], count(b, 1, 0))
                    dve.wait_ge(keep_ok, count(b, 1, 0))
                    nc.vector.scalar_tensor_tensor(
                        out=work[:, 0, :].rearrange("p (m n) -> p m n", m=QT),
                        in0=src[:].rearrange("p (m n) -> p m n", m=QT), scalar=0.0, in1=keep[:],
                        op0=ALU.max, op1=ALU.mult).then_inc(l1_masked, 1)
                elif name.startswith("av"):
                    dve.wait_ge(mm["av"], count(b, 2, k))
                    nc.vector.tensor_tensor(x1[:, k, :], src[:], x1[:, k, :], ALU.add
                                            ).then_inc(final, 1)

            def second_softmax(s, b):
                if s == AL_STEP + 1:
                    dve.wait_ge(l1_masked, count(b, 1, 0))
                    nc.vector.tensor_reduce(l1_max[:], work[:, 0, :].rearrange(
                        "p (m n) -> p m n", m=QT), AX.X, ALU.max, negate=True).then_inc(l1_maxed, 1)
                if s == AL_STEP + 2:
                    dve.wait_ge(l1_exped, count(b, 1, 0))
                    nc.vector.reciprocal(l1_rcp[:], l1_sum[:]).then_inc(l1_rcped, 1)
                if s == AL_STEP + 3:
                    dve.wait_ge(hi["e"], count(b, 1, 0))
                    for m in range(QT):
                        last = nc.vector.scalar_tensor_tensor(
                            out=eL[:, m, :], in0=work[:, 1, m * NODES:(m + 1) * NODES],
                            scalar=l1_rcp[:, m:m + 1], in1=eH[:, m, :].bitcast(f32),
                            op0=ALU.mult, op1=ALU.subtract)
                    last.then_inc(lo["e"], 1)

            def body(t, prev, cur, nxt, later):
                p, n = t - 1, t + 1
                present = {-1: prev, 0: cur, 1: nxt}
                for s in range(HEADS):
                    if prev and s == NORM2:
                        normalise(1, x1, work, p)
                    if prev:
                        second_softmax(s, p)
                    if cur and s + AHEAD < HEADS:
                        mask(s + AHEAD, t)
                    elif nxt and s + AHEAD >= HEADS:
                        if s + AHEAD == HEADS:
                            dve.wait_ge(far_next_ok, count(n, 1, 0))
                            if cur:
                                dve.wait_ge(masked, count(t, HEADS, HEADS - 1))
                            nc.vector.tensor_copy(far[:], far_next[:]).then_inc(far_ok, 1)
                        mask(s + AHEAD - HEADS, n)
                    if s == 0 and prev:
                        sum_parts(HEADS // 2 - 1, p)
                    elif s > 0 and s % 2 == 0 and cur:
                        sum_parts(s // 2 - 1, t)
                    if cur:
                        turned_low(s, t)
                    if s == VAR2 and prev:
                        aggregate(1, p)
                        reciprocal_deviation(p)
                    if s in STATS1 and later:
                        first_stats(STATS1.index(s), n + 1)
                    if s == NORM1 and cur and later:
                        normalise(0, xa, xa, n + 1)
                    for name in DENSE[s]:
                        if present[ROLE[name]] and not name.endswith("a"):
                            dense_low(tile(name), t + ROLE[name])
                        elif cur and not prev and tile(name) in SPARE and not name.endswith("a"):
                            merged_low(SPARE.index(tile(name)))
                    if nxt and not cur and s == step_of("h1_1"):
                        for c in range(FIRST, EARLY):
                            chunk_low(c)
                    if cur and not prev:
                        for c in range(EARLY, len(CHUNKS)):
                            if s == CHUNK_STEPS[c - EARLY]:
                                chunk_low(c)
                if later and not cur:
                    normalise(0, xa, xa, n + 1)

            for q in range(QT):
                first_stats(q, 0)
            dve.wait_ge(small_in, 64)
            nc.vector.tensor_scalar(bias_q[:], bias_q[:], -SCALE, None, ALU.mult
                                    ).then_inc(bias_q_ok, 1)
            bvH = eH[:, :, :].rearrange("p a (b m) -> p (a b) m", m=P)
            bvL = eL[:, :, :].rearrange("p a (b m) -> p (a b) m", m=P)
            bv_all = bias_v[:].unsqueeze(2).broadcast_to([P, KT, P])
            nc.vector.tensor_copy(bvH, bv_all).then_inc(bv_high, 1)
            dve.wait_ge(bv_high, 1)
            nc.vector.tensor_tensor(bvL, bv_all, bvH.bitcast(f32), ALU.subtract).then_inc(bv_low, 1)
            nc.vector.memset(val[:, :, :, 3 * HEAD:VPITCH], 1.0).then_inc(ones_ok, 1)
            for c in range(FIRST):
                if c == 2:
                    normalise(0, xa, xa, 0)
                chunk_low(c)
            sweep(dve, body)

        @block.gpsimd
        def _(pool):
            nc.gpsimd.memset(ident[:], 0.0).then_inc(ident_ok, 1)
            pool.wait_ge(ident_ok, 1)
            nc.gpsimd.affine_select(out=ident[:], in_=ident[:], compare_op=ALU.not_equal, fill=1.0,
                                    base=0, pattern=[[-1, P]], channel_multiplier=1
                                    ).then_inc(ident_ok, 1)

            def reciprocal_deviation(b):
                v, y = newton[0][:, 0, :], rstd[0][:]
                a, c = newton[0][:, 1, :], newton[0][:, 2, :]
                at = [0]

                def step(ins):
                    ins.then_inc(nstep[0], 1)
                    pool.wait_ge(nstep[0], count(b, NSTEPS[0], at[0]))
                    settle(pool, pool_settled)
                    at[0] += 1

                pool.wait_ge(var_ok[0], count(b, 1, 0))
                settle(pool, pool_settled)
                step(nc.gpsimd.tensor_scalar(v, meanvar[0][:, :, 1], EPS, None, ALU.add))
                step(nc.gpsimd.tensor_scalar(a, v.bitcast(i32), -0.5, float(RSQRT_SEED),
                                             ALU.mult, ALU.add))
                step(nc.gpsimd.tensor_copy(y.bitcast(i32), a))
                for _ in range(NEWTON_ROUNDS):
                    step(nc.gpsimd.tensor_tensor(a, y, y, ALU.mult))
                    step(nc.gpsimd.tensor_tensor(c, a, v, ALU.mult))
                    step(nc.gpsimd.tensor_scalar(a, c, -0.5, 1.5, ALU.mult, ALU.add))
                    step(nc.gpsimd.tensor_tensor(y, y, a, ALU.mult))

            def values_low(half, b):
                pool.wait_ge(v_mid, count(b, 2, half))
                heads = slice(8 * half, 8 * half + 8)
                rest = v_rest[:].rearrange("p q (h d) -> p q h d", d=HEAD)
                for q in range(QT):
                    last = nc.gpsimd.tensor_tensor(val[:, q, heads, 0:HEAD], rest[:, q, :, :],
                                                   val[:, q, heads, HEAD:2 * HEAD], ALU.subtract)
                last.then_inc(v_low, 1)

            def norm_heads(pair, b):
                pool.wait_ge(summed, count(b, HEADS // 2, pair))
                if started(b - 1):
                    pool.wait_ge(mm["ot"], count(b - 1, 2, pair // 4))
                for q in range(QT):
                    at = 2 * pair * HEAD
                    dst = heads_out[:, q, at:at + 2 * HEAD].rearrange("p (h d) -> p h d", h=2)
                    last = nc.gpsimd.tensor_tensor(
                        dst, o_sum[:, pair % 2, q:q + 3:2, :],
                        o_rcp[:, pair % 2, q:q + 3:2].unsqueeze(2).broadcast_to([P, 2, HEAD]),
                        ALU.mult)
                last.then_inc(head_ok, 1)

            def body(t, prev, cur, nxt, later):
                p, n = t - 1, t + 1
                for s in range(HEADS):
                    if s == VAR1 and later:
                        reciprocal_deviation(n + 1)
                    if s == MID[0] and nxt:
                        values_low(0, n)
                    if s == 0 and prev:
                        norm_heads(HEADS // 2 - 1, p)
                    elif s > 0 and s % 2 == 0 and cur:
                        norm_heads(s // 2 - 1, t)
                    if s == MID[1] and cur:
                        values_low(1, t)
                    if s == X1_STEP and prev and not started(p - 1):
                        pool.wait_ge(merged_lo, KT + 1)
                    if s == X1_STEP and prev:
                        pool.wait_ge(x1_in, count(p, 16, 15))
                        for q in range(QT):
                            last = nc.gpsimd.tensor_tensor(x1[:, q, :], x1[:, q, :], out_bias[:],
                                                           ALU.add)
                        last.then_inc(x1_ok, 1)
                    if s == KEEP_STEP and prev:
                        pool.wait_ge(adjt_got, count(p, 16, 15))
                        if started(p - 1):
                            pool.wait_ge(l1_masked, count(p - 1, 1, 0))
                        settle(pool, pool_settled)
                        for q in range(QT):
                            last = nc.gpsimd.tensor_scalar(keep[:, q, :], adjt_in[:, q, :], 0, 0,
                                                           ALU.is_equal, ALU.is_equal)
                        last.then_inc(keep_ok, 1)
                    if s == FAR_STEP and nxt:
                        pool.wait_ge(adj_got, count(n, 16, 15))
                        if started(t):
                            pool.wait_ge(far_ok, count(t, 1, 0))
                        settle(pool, pool_settled)
                        for q in range(QT):
                            last = nc.gpsimd.tensor_scalar(far_next[:, q, :], adj_in[:, q, :], 0,
                                                           FAR, ALU.is_equal, ALU.mult)
                        last.then_inc(far_next_ok, 1)

            reciprocal_deviation(0)
            pool.wait_ge(w_low, FIRST)
            sweep(pool, body)


def kernel(**inputs):
    import numpy as np
    import concourse.bacc as bacc
    from concourse.bass_utils import run_bass_kernel_spmd

    def columns(v):
        return np.ascontiguousarray(np.asarray(v).reshape(KT, P).T)

    src = {k: np.asarray(v) for k, v in inputs.items()}
    arrays = {
        "x": src["x"],
        "adj": src["adj"],
        "adj_t": np.ascontiguousarray(src["adj"].transpose(0, 2, 1)),
        "wq": src["L0_gnn_Wq"], "wk": src["L0_gnn_Wk"], "wv": src["L0_gnn_Wv"],
        "wo": src["L0_gnn_Wo"],
        "bq": columns(src["L0_gnn_bq"]), "bk": columns(src["L0_gnn_bk"]),
        "bv": columns(src["L0_gnn_bv"]), "bo": src["L0_gnn_bo"].reshape(1, DIM),
        "w1": src["L1_gnn_weight"],
        "wq1_t": np.ascontiguousarray(src["L1_gnn_wq"].T),
        "wk1_t": np.ascontiguousarray(src["L1_gnn_wk"].T),
    }
    nc = bacc.Bacc("TRN2", target_bir_lowering=False, num_devices=1)
    args = {n: nc.dram_tensor(f"{n}_dram", a.shape, mybir.dt.from_np(a.dtype),
                              kind="ExternalInput").ap() for n, a in arrays.items()}
    out = nc.dram_tensor("out_dram", (BATCH, NODES, DIM), mybir.dt.float32,
                         kind="ExternalOutput").ap()
    two_layers(nc, **args, out=out)
    r = run_bass_kernel_spmd(nc, [{f"{n}_dram": a for n, a in arrays.items()}], core_ids=[0])
    return r.results[0]["out_dram"]
```
